# Optimizing a Trainium2 kernel written in Bass

```python
import numpy as np
import jax
import jax.numpy as jnp

def _softmax(x, axis=-1):
    return jax.nn.softmax(x, axis=axis)

def _gelu(x):
    return jax.nn.gelu(x, approximate=True)

def _silu(x):
    return jax.nn.silu(x)

def _sigmoid(x):
    return jax.nn.sigmoid(x)

def _layernorm(x, axis=-1, eps=1e-05):
    m = jnp.mean(x, axis=axis, keepdims=True)
    v = jnp.var(x, axis=axis, keepdims=True)
    return (x - m) / jnp.sqrt(v + eps)

def _scatter_add(tgt, idx, src, axis=0):
    return tgt.at[idx].add(src)

def _segment_sum(src, seg, n):
    return jax.ops.segment_sum(src, seg, n)
kernel_name = 'mk_adj_resnorm_d2_adj_r2_c1d30c'

def setup_inputs(seed: int=0):
    np.random.seed(seed)
    _w = jnp.asarray

    def _rec_inputs():
        import jax
        import jax.numpy as jnp
        _gk = jax.random.key(seed)
        x = 7.22e-05 + 1 * jax.random.normal(jax.random.fold_in(_gk, 1), (64, 128, 256), jnp.float32)
        _w = (1.0 + jnp.arange(128, dtype=jnp.float32)) ** (-0.5)
        _w = _w / _w.mean()
        _pij = jnp.clip(0.03125 * _w[:, None] * _w[None, :], 0.0, 1.0)
        _a = jax.random.uniform(jax.random.fold_in(_gk, 2), (64, 128, 128)) < _pij
        _a = jnp.logical_or(_a, jnp.eye(128, dtype=bool))
        _af = _a.astype(jnp.float32)
        _af = _af * jax.random.uniform(jax.random.fold_in(_gk, 3), (64, 128, 128), jnp.float32, 0.05, 1)
        adj = _af
        _nm = jnp.ones((64, 128), dtype=bool)
        nodemask = jnp.where(_nm, 1.0, 0.0).astype(jnp.float32)
        return (x, adj, nodemask)
    x, adj, nodemask = _rec_inputs()

    def _L0_gnn_setup():
        import jax, jax.numpy as jnp
        import numpy as np
        B, N, IN_DIM, ATT_DIM = (2, 4096, 256, 256)
        key = jax.random.key(seed)
        k1, k2, k3, k4 = jax.random.split(key, 4)
        X = jax.random.normal(k1, (B, N, IN_DIM), dtype=jnp.float32)
        adj = jax.random.uniform(k2, (B, N, N), dtype=jnp.float32)
        mask = jnp.ones((B, N), dtype=jnp.float32)
        Wqk = jax.random.normal(k3, (IN_DIM, 2 * ATT_DIM), dtype=jnp.float32) / np.sqrt(IN_DIM)
        Wv = jax.random.normal(k4, (IN_DIM, IN_DIM), dtype=jnp.float32) / np.sqrt(IN_DIM)
        return {'X': X, 'adj': adj, 'mask': mask, 'Wqk': Wqk, 'Wv': Wv}
    _L0_gnn_all = _L0_gnn_setup()
    _L0_gnn_in = {k: v for k, v in _L0_gnn_all.items() if k in ('Wqk', 'Wv')}
    del _L0_gnn_all

    def _L1_gnn_setup():
        import jax, jax.numpy as jnp
        import numpy as np
        B, N, D = (8, 1024, 256)
        key = jax.random.key(seed)
        ks = jax.random.split(key, 8)
        scale = 0.5 / np.sqrt(D)
        x = jax.random.normal(ks[0], (B, N, D), dtype=jnp.float32)
        adj = jax.random.uniform(ks[1], (B, N, N), dtype=jnp.float32)
        Wq_w = jax.random.normal(ks[2], (D, D), dtype=jnp.float32) * scale
        Wk_w = jax.random.normal(ks[3], (D, D), dtype=jnp.float32) * scale
        Wv_w = jax.random.normal(ks[4], (D, D), dtype=jnp.float32) * scale
        Wq_b = jnp.zeros((D,), dtype=jnp.float32)
        Wk_b = jnp.zeros((D,), dtype=jnp.float32)
        Wv_b = jnp.zeros((D,), dtype=jnp.float32)
        return {'x': x, 'adj': adj, 'Wq_w': Wq_w, 'Wq_b': Wq_b, 'Wk_w': Wk_w, 'Wk_b': Wk_b, 'Wv_w': Wv_w, 'Wv_b': Wv_b}
    _L1_gnn_all = _L1_gnn_setup()
    _L1_gnn_in = {k: v for k, v in _L1_gnn_all.items() if k in ('Wq_w', 'Wq_b', 'Wk_w', 'Wk_b', 'Wv_w', 'Wv_b')}
    del _L1_gnn_all
    return {'x': x, 'adj': adj, 'nodemask': nodemask, 'L0_gnn_Wqk': _L0_gnn_in['Wqk'], 'L0_gnn_Wv': _L0_gnn_in['Wv'], 'L1_gnn_Wq_w': _L1_gnn_in['Wq_w'], 'L1_gnn_Wq_b': _L1_gnn_in['Wq_b'], 'L1_gnn_Wk_w': _L1_gnn_in['Wk_w'], 'L1_gnn_Wk_b': _L1_gnn_in['Wk_b'], 'L1_gnn_Wv_w': _L1_gnn_in['Wv_w'], 'L1_gnn_Wv_b': _L1_gnn_in['Wv_b']}

def reference(x, adj, nodemask, L0_gnn_Wqk, L0_gnn_Wv, L1_gnn_Wq_w, L1_gnn_Wq_b, L1_gnn_Wk_w, L1_gnn_Wk_b, L1_gnn_Wv_w, L1_gnn_Wv_b):
    import jax
    import jax.numpy as jnp

    def _L0_gnn_ref(X, adj, mask, Wqk, Wv):
        import jax, jax.numpy as jnp
        import numpy as np
        B, N, IN_DIM, ATT_DIM = (2, 4096, 256, 256)
        qk = X @ Wqk
        q, k = jnp.split(qk, 2, axis=-1)
        v = X @ Wv
        att_dim = q.shape[-1]
        inv_scale = 1.0 / jnp.sqrt(jnp.float32(att_dim))
        k_m = k * mask[:, :, None]
        agg = jnp.einsum('bij,bjd->bid', adj, k_m)
        w = inv_scale * mask * jnp.einsum('bid,bid->bi', q, agg)
        L = jax.nn.softmax(w, axis=1)[:, :, None] * v
        return L

    def _L1_gnn_ref(x, adj, Wq_w, Wq_b, Wk_w, Wk_b, Wv_w, Wv_b):
        import jax, jax.numpy as jnp
        import numpy as np
        B, N, D = (8, 1024, 256)
        query = jnp.einsum('bnd,od->bno', x, Wq_w) + Wq_b
        keyt = jnp.einsum('bnd,od->bno', x, Wk_w) + Wk_b
        value = jnp.einsum('bnd,od->bno', x, Wv_w) + Wv_b
        weight = jnp.einsum('bqd,bkd->bqk', query, keyt)
        weight = adj * jnp.exp(weight)
        weight = weight / jnp.sum(weight, axis=2, keepdims=True)
        return jnp.einsum('bqk,bkd->bqd', weight, value)
    x = _layernorm(x + _L0_gnn_ref(x, adj, nodemask, L0_gnn_Wqk, L0_gnn_Wv), axis=-1)
    x = _layernorm(x + _L1_gnn_ref(x, adj, L1_gnn_Wq_w, L1_gnn_Wq_b, L1_gnn_Wk_w, L1_gnn_Wk_b, L1_gnn_Wv_w, L1_gnn_Wv_b), axis=-1)
    return x

_drawn_inputs = setup_inputs


def setup_inputs(seed=0):
    import zlib

    import numpy as np

    out = dict(_drawn_inputs(seed))
    spreads = {'L1_gnn_Wq_b': (0.0, 0.1), 'L1_gnn_Wk_b': (0.0, 0.1), 'L1_gnn_Wv_b': (0.0, 0.1)}
    factors = {}
    for name, (base, spread) in spreads.items():
        noise = np.random.default_rng([zlib.crc32(name.encode()), seed]).standard_normal(out[name].shape)
        drawn = base * np.exp(spread * noise) if base else spread * noise
        out[name] = jnp.asarray(drawn.astype(out[name].dtype))
    for name, factor in factors.items():
        out[name] = (out[name] * factor).astype(out[name].dtype)
    return out
```

```python
from contextlib import ExitStack

import concourse.bass as bass
from concourse import mybir

F32 = mybir.dt.float32
F32R = mybir.dt.float32r
ALU = mybir.AluOpType
ACT = mybir.ActivationFunctionType
AX = mybir.AxisListType

GRAPHS, NODES, DIM = 64, 128, 256
HALVES = DIM // 128
PAIRS = GRAPHS // 2
PAIR_X = 2 * DIM
PAIR_N = 2 * NODES
ADJ_COLS = PAIR_N + 2
VAL_COLS = DIM + 2
EPS = 1e-5
ATT_SCALE = 1.0 / 16.0
P0_COLS = 4 * DIM + HALVES * DIM
P1_COLS = 3 * HALVES * DIM + 2 * HALVES
LOOP_FROM, LOOP_TO, UNROLL = 3, 27, 4
FIRST, LAST = -3, PAIRS + 1


def exists(pair):
    return not isinstance(pair, int) or 0 <= pair < PAIRS


def build(nc, x_pairs, xt_pairs, adjt_pairs, params0, params1, value_bias, out_pairs):
    ctx = ExitStack()
    with ctx:
        def sb(name, shape, dt=F32):
            return ctx.enter_context(nc.sbuf_tensor(name, shape, dt))

        def sem(name):
            return ctx.enter_context(nc.semaphore(name))

        def sems(name, n):
            return [sem(f"{name}{i}") for i in range(n)]

        p0 = sb("p0", [128, P0_COLS])
        p1 = sb("p1", [128, P1_COLS])
        wqkT = p0[:, 0:4 * DIM].rearrange("p (t a) -> p t a", t=4)
        wv0 = p0[:, 4 * DIM:P0_COLS].rearrange("p (t a) -> p t a", t=HALVES)
        wq1, wk1, wv1T = (p1[:, n * 2 * DIM:(n + 1) * 2 * DIM].rearrange("p (t a) -> p t a", t=HALVES)
                          for n in range(3))
        bq = p1[:, 6 * DIM:6 * DIM + 2]
        bk = p1[:, 6 * DIM + 2:6 * DIM + 4]
        bq_wide = sb("bq_wide", [128, HALVES, 128])
        bv_all = sb("bv_all", [128, DIM])
        ident = sb("ident", [128, 128])
        minus_half = sb("minus_half", [128, 4])
        w0_hi = sb("w0_hi", [128, HALVES, 2 * DIM], F32R)
        w0_lo = sb("w0_lo", [128, HALVES, 2 * DIM], F32R)
        at_hi = sb("at_hi", [128, HALVES, DIM], F32R)
        at_lo = sb("at_lo", [128, HALVES, DIM], F32R)
        wv1_hi = sb("wv1_hi", [128, HALVES, VAL_COLS], F32R)
        wv1_lo = sb("wv1_lo", [128, HALVES, VAL_COLS], F32R)
        z_bias = sb("z_bias", [128, HALVES])
        s_bias = sb("s_bias", [128, 1])

        x_raw = [sb(f"x_raw{i}", [128, PAIR_X]) for i in range(4)]
        adjt = [sb(f"adjt{i}", [128, ADJ_COLS]) for i in range(4)]
        xt_raw = [sb(f"xt_raw{i}", [128, PAIR_X]) for i in range(2)]
        xt_hi = [sb(f"xt_hi{i}", [128, HALVES, 2, 128], F32R) for i in range(4)]
        xt_lo = [sb(f"xt_lo{i}", [128, HALVES, 2, 128], F32R) for i in range(4)]
        x_hi = [sb(f"x_hi{i}", [128, PAIR_X], F32R) for i in range(2)]
        x_lo = [sb(f"x_lo{i}", [128, PAIR_X], F32R) for i in range(2)]
        adjm = sb("adjm", [128, PAIR_N])
        adjm_hi = [sb(f"adjm_hi{i}", [128, PAIR_N], F32R) for i in range(2)]
        adjm_lo = [sb(f"adjm_lo{i}", [128, PAIR_N], F32R) for i in range(2)]
        agg = sb("agg", [128, 2, DIM])
        w_col = [sb(f"w_col{i}", [128, 2]) for i in range(2)]
        neg_max = sb("neg_max", [2, 1])
        exp_sum = sb("exp_sum", [2, 1])
        exp_row = sb("exp_row", [2, 128])
        inv_sum = sb("inv_sum", [2, 1])
        inv_diag = sb("inv_diag", [2, 2])
        p_col = sb("p_col", [128, 2])
        x1_sum = [sb(f"x1_sum{i}", [128, PAIR_X]) for i in range(2)]
        x1 = [sb(f"x1_{i}", [128, PAIR_X]) for i in range(2)]
        x1b = [sb(f"x1b{i}", [128, PAIR_X]) for i in range(2)]
        x1t_hi = sb("x1t_hi", [128, HALVES, 2, 128], F32R)
        x1t_lo = sb("x1t_lo", [128, HALVES, 2, 128], F32R)
        z_hi = sb("z_hi", [128, HALVES, PAIR_N], F32R)
        z_lo = sb("z_lo", [128, HALVES, PAIR_N], F32R)
        val = sb("val", [128, 2, VAL_COLS])
        score_bias = sb("score_bias", [128, 2])
        exp_s = sb("exp_s", [128, PAIR_N])
        edge = sb("edge", [128, PAIR_N])
        den_inv = sb("den_inv", [128, 2])
        x2 = [sb(f"x2_{i}", [128, PAIR_X]) for i in range(4)]
        stats1 = sb("stats1", [128, 2, 6])
        stats2 = sb("stats2", [128, 2, 6])
        mean_var = sb("mean_var", [128, 4, 2])
        var_eps = sb("var_eps", [128, 4])
        rstd = sb("rstd", [128, 4])
        shift = sb("shift", [128, 4])

        ps = ctx.enter_context(nc.psum_tensor("ps", [128, 8, 512], F32))
        x1t_ps = ps[:, 0, :].rearrange("p (t g n) -> p t g n", t=HALVES, g=2)
        z_ps = ps[:, 0, :].rearrange("p (t n) -> p t n", t=HALVES)
        sum_ps = ps[:, 1:3, :]
        score_ps = ps[:, 1:3, 384:512]
        val_ps = ps[:, 3:5, :]
        w_row_ps = ps[0:2, 3, 384:512]
        p_col_ps = ps[:, 4, 384:386]
        y_ps = ps[:, 5:7, 0:DIM]
        agg_ps = ps[:, 5:7, DIM:2 * DIM]
        v0_ps = ps[:, 7, :].rearrange("p (g d) -> p g d", g=2)
        m0_ps = ps[:, 5, :].rearrange("p (t a) -> p t a", t=HALVES)
        at_ps = ps[:, 6, :].rearrange("p (t a) -> p t a", t=HALVES)
        bias_ps = ps[:, 7, :]

        params0_loaded, params1_loaded, bv_loaded = sem("params0_loaded"), sem("params1_loaded"), sem("bv_loaded")
        x_loaded, adj_loaded, xt_loaded = sems("x_loaded", 4), sems("adj_loaded", 4), sems("xt_loaded", 2)
        out_stored = sems("out_stored", 4)
        ident_zeroed, ident_ready, consts_ready = sem("ident_zeroed"), sem("ident_ready"), sem("consts_ready")
        bq_widened = sem("bq_widened")
        m0_done, at_done, bias_done = sem("m0_done"), sem("at_done"), sem("bias_done")
        w0_hi_done, w0_lo_done, w1_hi_done, w1_lo_done = sem("w0_hi_done"), sem("w0_lo_done"), sem("w1_hi_done"), sem("w1_lo_done")
        y_done = sems("y_done", 2)
        x1t_done, w_row_done, p_col_done, v0_done = sem("x1t_done"), sem("w_row_done"), sem("p_col_done"), sem("v0_done")
        sum_done, z_done, val_done, score_done = sem("sum_done"), sem("z_done"), sem("val_done"), sem("score_done")
        xt_hi_done, x_hi_done, adjm_hi_done = sem("xt_hi_done"), sem("x_hi_done"), sem("adjm_hi_done")
        agg_copied = sems("agg_copied", 2)
        x1t_hi_done, row_exp_done, z_hi_done = sem("x1t_hi_done"), sem("row_exp_done"), sem("z_hi_done")
        val_copied, score_exp_done, x1_done, out_done = sem("val_copied"), sem("score_exp_done"), sem("x1_done"), sem("out_done")
        w_done = sems("w_done", 2)
        row_max_done, inv_sum_done, inv_diag_done, p_copied = sem("row_max_done"), sem("inv_sum_done"), sem("inv_diag_done"), sem("p_copied")
        x1_sum_done, stats1_done, x1t_lo_done, z_lo_done = sem("x1_sum_done"), sem("stats1_done"), sem("x1t_lo_done"), sem("z_lo_done")
        score_bias_done, edge_done, den_inv_done = sem("score_bias_done"), sem("edge_done"), sem("den_inv_done")
        x2_done, stats2_done = sem("x2_done"), sem("stats2_done")
        norms_ready = sem("norms_ready")
        mean_var_done, var_eps_done, shift_done = sem("mean_var_done"), sem("var_eps_done"), sem("shift_done")
        xt_lo_done, x_lo_done, adjm_done, adjm_lo_done = sem("xt_lo_done"), sem("x_lo_done"), sem("adjm_done"), sem("adjm_lo_done")
        x1b_done, rstd_done = sem("x1b_done"), sem("rstd_done")

        def graph(g, width=DIM):
            return slice(g * width, (g + 1) * width)

        def transfers4(u, r):
            return 4 * (u - r % 4) + 16

        def transfers2(u, r):
            return 8 * (u - r % 2) + 16

        def norms(t):
            return t + 2

        def slots(eng, slot):
            for t in range(FIRST, LOOP_FROM):
                slot(t, t)
            with eng.Fori(LOOP_FROM, LOOP_TO - UNROLL + 1, UNROLL) as base:
                for j in range(UNROLL):
                    slot(base + j, LOOP_FROM + j)
            for t in range(LOOP_TO, LAST + 1):
                slot(t, t)

        block = ctx.enter_context(nc.Block())

        @block.sync
        def _(sp):
            def load_x(u, r):
                sp.dma_start(x_raw[r % 4][:, :], x_pairs[u]).then_inc(x_loaded[r % 4], 16)

            def load_xt(u, r):
                sp.dma_start(xt_raw[r % 2][:, :], xt_pairs[u]).then_inc(xt_loaded[r % 2], 16)

            def load_adj(u, r):
                sp.dma_start(adjt[r % 4][:, :], adjt_pairs[u]).then_inc(adj_loaded[r % 4], 16)

            def slot(t, r):
                if exists(t + 3) and exists(t - 1):
                    sp.wait_ge(edge_done, t)
                    load_adj(t + 3, r + 3)
                if exists(t + 4) and exists(t + 2):
                    sp.wait_ge(xt_lo_done, t + 3)
                    load_xt(t + 4, r + 4)
                if exists(t + 4) and exists(t):
                    sp.wait_ge(x1_sum_done, t + 1)
                    load_x(t + 4, r + 4)
                if exists(t - 2):
                    sp.wait_ge(out_done, t - 1)
                    sp.dma_start(out_pairs[t - 2], x2[(r - 2) % 4][:, :]).then_inc(out_stored[(r - 2) % 4], 16)

            sp.dma_start(p0[:, :], params0).then_inc(params0_loaded, 16)
            for u in range(2):
                load_adj(u, u)
                load_xt(u, u)
                load_x(u, u)
                if u == 0:
                    sp.dma_start(p1[:, :], params1).then_inc(params1_loaded, 16)
                    sp.dma_start(bv_all[:, :], value_bias.partition_broadcast(128)).then_inc(bv_loaded, 16)
            for u in range(2, 4):
                load_adj(u, u)
                load_x(u, u)
            for q in out_stored:
                sp.sem_inc(q, 16)
            slots(sp, slot)
            for q in out_stored:
                sp.wait_ge(q, 16 + 16 * PAIRS // 4)

        @block.gpsimd
        def _(pool):
            def slot(t, r):
                if exists(t):
                    pool.wait_ge(x1_done, t + 1)
                    if isinstance(t, int) and t == 0:
                        pool.wait_ge(bv_loaded, 16)
                    nc.gpsimd.tensor_tensor(
                        x1b[r % 2][:, :].rearrange("p (g d) -> p g d", g=2),
                        x1[r % 2][:, :].rearrange("p (g d) -> p g d", g=2),
                        bv_all[:, :].unsqueeze(1).broadcast_to([128, 2, DIM]), ALU.add).then_inc(x1b_done, 1)
                if exists(t + 3):
                    pool.wait_ge(adj_loaded[(r + 3) % 4], transfers4(t + 3, r + 3))
                    if exists(t + 2):
                        pool.wait_ge(adjm_lo_done, t + 3)
                    a = adjt[(r + 3) % 4]
                    nc.gpsimd.tensor_tensor(
                        adjm[:, :].rearrange("p (g n) -> p g n", g=2),
                        a[:, 0:PAIR_N].rearrange("p (g n) -> p g n", g=2),
                        a[:, PAIR_N:ADJ_COLS].unsqueeze(2).broadcast_to([128, 2, NODES]), ALU.mult)\
                        .then_inc(adjm_done, 1)
                    pool.wait_ge(xt_hi_done, t + 4)
                    nc.gpsimd.tensor_tensor(
                        xt_lo[(r + 3) % 4][:, :, :, :].rearrange("p t g n -> p (t g n)"), xt_raw[(r + 3) % 2][:, :],
                        xt_hi[(r + 3) % 4][:, :, :, :].rearrange("p t g n -> p (t g n)").bitcast(F32), ALU.subtract)\
                        .then_inc(xt_lo_done, 1)
                    pool.wait_ge(x_hi_done, t + 4)
                    nc.gpsimd.tensor_tensor(x_lo[(r + 3) % 2][:, :], x_raw[(r + 3) % 4][:, :],
                                            x_hi[(r + 3) % 2][:, :].bitcast(F32), ALU.subtract).then_inc(x_lo_done, 1)
                if exists(t + 1) or exists(t - 2):
                    pool.wait_ge(var_eps_done, norms(t))
                    if exists(t):
                        pool.wait_ge(x1_done, t + 1)
                    if exists(t - 3):
                        pool.wait_ge(out_done, t - 2)
                    nc.gpsimd.tensor_tensor(rstd[:, :], var_eps[:, :], minus_half[:, :], ALU.pow).then_inc(rstd_done, 1)
                if exists(t + 3):
                    pool.wait_ge(adjm_hi_done, t + 4)
                    nc.gpsimd.tensor_tensor(adjm_lo[(r + 3) % 2][:, :], adjm[:, :],
                                            adjm_hi[(r + 3) % 2][:, :].bitcast(F32), ALU.subtract).then_inc(adjm_lo_done, 1)

            nc.gpsimd.memset(ident[:, :], 0.0).then_inc(ident_zeroed, 1)
            nc.gpsimd.memset(minus_half[:, :], -0.5)
            nc.gpsimd.memset(wv1_hi[:, :, DIM:VAL_COLS].bitcast(F32), 0.0)
            nc.gpsimd.memset(wv1_lo[:, :, DIM:VAL_COLS].bitcast(F32), 0.0)
            nc.gpsimd.memset(val[:, :, DIM:DIM + 1], 1.0)
            nc.gpsimd.memset(val[:, :, DIM + 1:VAL_COLS], 0.0).then_inc(consts_ready, 1)
            pool.wait_ge(ident_zeroed, 1)
            nc.gpsimd.affine_select(out=ident[:, :], in_=ident[:, :], compare_op=ALU.not_equal, fill=1.0, base=0,
                                    pattern=[[-1, 128]], channel_multiplier=1).then_inc(ident_ready, 1)
            pool.wait_ge(consts_ready, 1)
            slots(pool, slot)

        @block.scalar
        def _(act):
            def copy_agg(u, g):
                act.wait_ge(y_done[g], u + 1)
                if exists(u - 1):
                    act.wait_ge(w_done[g], u)
                nc.scalar.copy(agg[:, g, :], agg_ps[:, g, :]).then_inc(agg_copied[g], 1)

            def norm(out, in_, first, done):
                for g in range(2):
                    n = first + g
                    last = nc.scalar.activation(out[:, graph(g)], in_[:, graph(g)], ACT.Identity,
                                                bias=shift[:, n:n + 1], scale=rstd[:, n:n + 1])
                last.then_inc(done, 1)

            def slot(t, r):
                if exists(t - 1):
                    act.wait_ge(score_done, t)
                    act.wait_ge(score_bias_done, t)
                    if exists(t - 2):
                        act.wait_ge(edge_done, t - 1)
                    for g in range(2):
                        last = nc.scalar.activation(exp_s[:, graph(g, NODES)], score_ps[:, g, :], ACT.Exp,
                                                    bias=score_bias[:, g:g + 1])
                    last.then_inc(score_exp_done, 1)
                if exists(t):
                    act.wait_ge(x1t_done, t + 1)
                    nc.scalar.copy(x1t_hi[:, :, :, :], x1t_ps).then_inc(x1t_hi_done, 1)
                if exists(t + 1):
                    act.wait_ge(row_max_done, t + 2)
                    nc.scalar.activation(exp_row[:, :], w_row_ps, ACT.Exp, bias=neg_max[:, 0:1],
                                         accum_out=exp_sum[:, 0:1]).then_inc(row_exp_done, 1)
                if exists(t + 3):
                    act.wait_ge(xt_loaded[(r + 3) % 2], transfers2(t + 3, r + 3))
                    if exists(t - 1):
                        act.wait_ge(v0_done, t)
                    nc.scalar.copy(xt_hi[(r + 3) % 4][:, :, :, :].rearrange("p t g n -> p (t g n)"),
                                   xt_raw[(r + 3) % 2][:, :]).then_inc(xt_hi_done, 1)
                    act.wait_ge(x_loaded[(r + 3) % 4], transfers4(t + 3, r + 3))
                    if exists(t + 1):
                        act.wait_ge(y_done[1], t + 2)
                    nc.scalar.copy(x_hi[(r + 3) % 2][:, :], x_raw[(r + 3) % 4][:, :]).then_inc(x_hi_done, 1)
                    act.wait_ge(adjm_done, t + 4)
                    nc.scalar.copy(adjm_hi[(r + 3) % 2][:, :], adjm[:, :]).then_inc(adjm_hi_done, 1)
                if exists(t):
                    act.wait_ge(z_done, t + 1)
                    for m in range(HALVES):
                        last = nc.scalar.activation(z_hi[:, m, :], z_ps[:, m, :], ACT.Identity, bias=z_bias[:, m:m + 1])
                    last.then_inc(z_hi_done, 1)
                if exists(t + 2):
                    copy_agg(t + 2, 0)
                if exists(t + 1):
                    act.wait_ge(shift_done, norms(t))
                    if exists(t - 1):
                        act.wait_ge(x1b_done, t)
                    norm(x1[(r + 1) % 2], x1_sum[(r + 1) % 2], 0, x1_done)
                if exists(t):
                    act.wait_ge(val_done, t + 1)
                    nc.scalar.copy(val[:, :, 0:DIM], val_ps[:, :, 0:DIM]).then_inc(val_copied, 1)
                if exists(t + 2):
                    copy_agg(t + 2, 1)
                if exists(t - 2):
                    act.wait_ge(shift_done, norms(t))
                    norm(x2[(r - 2) % 4], x2[(r - 2) % 4], 2, out_done)

            act.wait_ge(params0_loaded, 16)
            nc.scalar.copy(w0_hi[:, :, DIM:2 * DIM], wv0)
            act.wait_ge(m0_done, 1)
            nc.scalar.activation(w0_hi[:, :, 0:DIM], m0_ps, ACT.Copy, scale=ATT_SCALE).then_inc(w0_hi_done, 1)
            act.wait_ge(params1_loaded, 16)
            act.wait_ge(consts_ready, 1)
            nc.scalar.copy(wv1_hi[:, :, 0:DIM], wv1T)
            act.wait_ge(at_done, 1)
            nc.scalar.copy(at_hi[:, :, :], at_ps)
            act.wait_ge(bias_done, 1)
            nc.scalar.copy(wv1_hi[:, :, DIM], bias_ps[:, 2:4]).then_inc(w1_hi_done, 1)
            slots(act, slot)

        @block.vector
        def _(dve):
            def weight(u, r, g):
                dve.wait_ge(agg_copied[g], u + 1)
                if exists(u - 2):
                    dve.wait_ge(w_row_done, u - 1)
                nc.vector.tensor_tensor_reduce(agg[:, g, :], y_ps[:, g, :], agg[:, g, :],
                                               adjt[r % 4][:, PAIR_N + g:PAIR_N + g + 1], 0.0, ALU.mult, ALU.add,
                                               w_col[r % 2][:, g:g + 1]).then_inc(w_done[g], 1)

            def slot(t, r):
                if exists(t + 1):
                    dve.wait_ge(w_row_done, t + 2)
                    nc.vector.tensor_reduce(neg_max[:, :], w_row_ps, AX.X, ALU.max, negate=True).then_inc(row_max_done, 1)
                if exists(t - 1):
                    dve.wait_ge(score_exp_done, t)
                    if exists(t - 2):
                        dve.wait_ge(sum_done, t - 1)
                    nc.vector.tensor_tensor(edge[:, :], exp_s[:, :], adjt[(r - 1) % 4][:, 0:PAIR_N], ALU.mult)\
                        .then_inc(edge_done, 1)
                if exists(t):
                    dve.wait_ge(x1t_hi_done, t + 1)
                    nc.vector.tensor_tensor(x1t_lo[:, :, :, :], x1t_ps, x1t_hi[:, :, :, :].bitcast(F32), ALU.subtract)\
                        .then_inc(x1t_lo_done, 1)
                if exists(t + 1):
                    dve.wait_ge(row_exp_done, t + 2)
                    nc.vector.reciprocal(inv_sum[:, :], exp_sum[:, :]).then_inc(inv_sum_done, 1)
                    dve.wait_ge(inv_sum_done, t + 2)
                    nc.vector.tensor_scalar(inv_diag[:, :], ident[0:2, 0:2], inv_sum[:, 0:1], None, ALU.mult)\
                        .then_inc(inv_diag_done, 1)
                if exists(t - 1):
                    dve.wait_ge(sum_done, t)
                    nc.vector.reciprocal(den_inv[:, :], sum_ps[:, :, DIM]).then_inc(den_inv_done, 1)
                    dve.wait_ge(x1b_done, t)
                    dve.wait_ge(out_stored[(r - 1) % 4], transfers4(t - 1, r - 1))
                    dve.wait_ge(den_inv_done, t)
                    for g in range(2):
                        last = nc.vector.scalar_tensor_tensor(
                            out=x2[(r - 1) % 4][:, graph(g)], in0=sum_ps[:, g, 0:DIM], scalar=den_inv[:, g:g + 1],
                            in1=x1b[(r - 1) % 2][:, graph(g)], op0=ALU.mult, op1=ALU.add)
                    last.then_inc(x2_done, 1)
                if exists(t + 1):
                    dve.wait_ge(p_col_done, t + 2)
                    if exists(t):
                        dve.wait_ge(x1_sum_done, t + 1)
                    nc.vector.tensor_copy(p_col[:, :], p_col_ps).then_inc(p_copied, 1)
                    dve.wait_ge(v0_done, t + 2)
                    if exists(t - 1):
                        dve.wait_ge(x1_done, t)
                    dve.wait_ge(p_copied, t + 2)
                    for g in range(2):
                        last = nc.vector.scalar_tensor_tensor(
                            out=x1_sum[(r + 1) % 2][:, graph(g)], in0=v0_ps[:, g, :], scalar=p_col[:, g:g + 1],
                            in1=x_raw[(r + 1) % 4][:, graph(g)], op0=ALU.mult, op1=ALU.add)
                    last.then_inc(x1_sum_done, 1)
                    dve.wait_ge(x1_sum_done, t + 2)
                    for g in range(2):
                        last = nc.vector.bn_stats(stats1[:, g, :], x1_sum[(r + 1) % 2][:, graph(g)])
                    last.then_inc(stats1_done, 1)
                if exists(t + 1) or exists(t - 2):
                    dve.wait_ge(norms_ready, 1)
                    if exists(t):
                        dve.wait_ge(shift_done, norms(t) - 1)
                    if exists(t + 1):
                        dve.wait_ge(stats1_done, t + 2)
                    if exists(t - 2):
                        dve.wait_ge(stats2_done, t - 1)
                    for g in range(2):
                        if exists(t + 1):
                            last = nc.vector.bn_aggr(mean_var[:, g, :], stats1[:, g, :])
                        if exists(t - 2):
                            last = nc.vector.bn_aggr(mean_var[:, 2 + g, :], stats2[:, g, :])
                    last.then_inc(mean_var_done, 1)
                    dve.wait_ge(mean_var_done, norms(t))
                    nc.vector.tensor_scalar(var_eps[:, :], mean_var[:, :, 1], EPS, None, ALU.add).then_inc(var_eps_done, 1)
                if exists(t):
                    dve.wait_ge(z_hi_done, t + 1)
                    for m in range(HALVES):
                        last = nc.vector.scalar_tensor_tensor(
                            out=z_lo[:, m, :], in0=z_ps[:, m, :], scalar=z_bias[:, m:m + 1],
                            in1=z_hi[:, m, :].bitcast(F32), op0=ALU.add, op1=ALU.subtract)
                    last.then_inc(z_lo_done, 1)
                if exists(t + 2):
                    weight(t + 2, r + 2, 0)
                if exists(t + 1) or exists(t - 2):
                    dve.wait_ge(rstd_done, norms(t))
                    nc.vector.scalar_tensor_tensor(out=shift[:, :], in0=mean_var[:, :, 0], scalar=-1.0, in1=rstd[:, :],
                                                   op0=ALU.mult, op1=ALU.mult).then_inc(shift_done, 1)
                if exists(t - 1):
                    dve.wait_ge(x2_done, t)
                    for g in range(2):
                        last = nc.vector.bn_stats(stats2[:, g, :], x2[(r - 1) % 4][:, graph(g)])
                    last.then_inc(stats2_done, 1)
                if exists(t):
                    dve.wait_ge(val_copied, t + 1)
                    nc.vector.tensor_scalar(score_bias[:, :], val_ps[:, :, DIM], s_bias[:, 0:1], None, ALU.add)\
                        .then_inc(score_bias_done, 1)
                if exists(t + 2):
                    weight(t + 2, r + 2, 1)

            nc.vector.memset(mean_var[:, :, :], 1.0).then_inc(norms_ready, 1)
            dve.wait_ge(w0_hi_done, 1)
            nc.vector.tensor_tensor(w0_lo[:, :, DIM:2 * DIM], wv0, w0_hi[:, :, DIM:2 * DIM].bitcast(F32), ALU.subtract)
            nc.vector.scalar_tensor_tensor(
                out=w0_lo[:, :, 0:DIM], in0=m0_ps, scalar=ATT_SCALE,
                in1=w0_hi[:, :, 0:DIM].bitcast(F32), op0=ALU.mult, op1=ALU.subtract).then_inc(w0_lo_done, 1)
            dve.wait_ge(params1_loaded, 16)
            nc.vector.tensor_copy(bq_wide[:, :, :], bq.unsqueeze(2).broadcast_to([128, HALVES, 128])).then_inc(bq_widened, 1)
            dve.wait_ge(w1_hi_done, 1)
            dve.wait_ge(norms_ready, 1)
            nc.vector.tensor_tensor(wv1_lo[:, :, 0:DIM], wv1T, wv1_hi[:, :, 0:DIM].bitcast(F32), ALU.subtract)
            nc.vector.tensor_tensor(at_lo[:, :, :], at_ps, at_hi[:, :, :].bitcast(F32), ALU.subtract)
            nc.vector.tensor_tensor(wv1_lo[:, :, DIM], bias_ps[:, 2:4], wv1_hi[:, :, DIM].bitcast(F32), ALU.subtract)
            nc.vector.tensor_copy(z_bias[:, :], bias_ps[:, 0:2])
            nc.vector.tensor_copy(s_bias[:, :], bias_ps[:, 4:5]).then_inc(w1_lo_done, 1)
            dve.wait_ge(w1_lo_done, 1)
            dve.wait_ge(ident_ready, 1)
            slots(dve, slot)

        @block.tensor
        def _(pe):
            def split_product(out, parts):
                for n, (s_hi, s_lo, m_hi, m_lo) in enumerate(parts):
                    nc.tensor.matmul(out, s_hi, m_hi, start=(n == 0), stop=False)
                    nc.tensor.matmul(out, s_hi, m_lo, start=False, stop=False)
                    mm = nc.tensor.matmul(out, s_lo, m_hi, start=False, stop=(n == len(parts) - 1))
                return mm

            def layer0(u, r, g):
                pe.wait_ge(adjm_lo_done, u + 1)
                if exists(u - 1):
                    pe.wait_ge(w_done[g], u)
                n = graph(g, NODES)
                split_product(agg_ps[:, g, :], [(adjm_hi[r % 2][:, n], adjm_lo[r % 2][:, n],
                                                 x_hi[r % 2][:, graph(g)], x_lo[r % 2][:, graph(g)])])
                split_product(y_ps[:, g, :], [(xt_hi[r % 4][:, k, g, :], xt_lo[r % 4][:, k, g, :],
                                               w0_hi[:, k, 0:DIM], w0_lo[:, k, 0:DIM]) for k in range(HALVES)])\
                    .then_inc(y_done[g], 1)

            def slot(t, r):
                if exists(t):
                    pe.wait_ge(x1_done, t + 1)
                    if exists(t - 1):
                        pe.wait_ge(z_lo_done, t)
                    for g in range(2):
                        for k in range(HALVES):
                            c = g * DIM + k * 128
                            mm = nc.tensor.transpose(x1t_ps[:, k, g, :], x1[r % 2][:, c:c + 128], ident[:, :])
                    mm.then_inc(x1t_done, 1)
                if exists(t + 1):
                    if exists(t - 1):
                        pe.wait_ge(score_bias_done, t)
                    for g in range(2):
                        pe.wait_ge(w_done[g], t + 2)
                    nc.tensor.transpose(w_row_ps, w_col[(r + 1) % 2][:, :], ident[:, :]).then_inc(w_row_done, 1)
                    if exists(t):
                        pe.wait_ge(x1_sum_done, t + 1)
                    for g in range(2):
                        mm = split_product(v0_ps[:, g, :], [(
                            xt_hi[(r + 1) % 4][:, k, g, :], xt_lo[(r + 1) % 4][:, k, g, :],
                            w0_hi[:, k, DIM:2 * DIM], w0_lo[:, k, DIM:2 * DIM]) for k in range(HALVES)])
                    mm.then_inc(v0_done, 1)
                if exists(t - 1):
                    pe.wait_ge(edge_done, t)
                    pe.wait_ge(val_copied, t)
                    for g in range(2):
                        mm = nc.tensor.matmul(sum_ps[:, g, 0:VAL_COLS], edge[:, graph(g, NODES)], val[:, g, :],
                                              start=True, stop=True)
                    mm.then_inc(sum_done, 1)
                if exists(t + 1):
                    pe.wait_ge(inv_diag_done, t + 2)
                    if exists(t):
                        pe.wait_ge(p_copied, t + 1)
                    nc.tensor.matmul(p_col_ps, exp_row[:, :], inv_diag[:, :], start=True, stop=True).then_inc(p_col_done, 1)
                if exists(t):
                    pe.wait_ge(x1t_lo_done, t + 1)
                    for m in range(HALVES):
                        c = slice(m * 128, (m + 1) * 128)
                        mm = split_product(z_ps[:, m, :], [(
                            at_hi[:, k, c], at_lo[:, k, c], x1t_hi[:, k, :, :].rearrange("p g n -> p (g n)"),
                            x1t_lo[:, k, :, :].rearrange("p g n -> p (g n)")) for k in range(HALVES)])
                    mm.then_inc(z_done, 1)
                if exists(t + 2):
                    layer0(t + 2, r + 2, 0)
                if exists(t):
                    if exists(t + 1):
                        pe.wait_ge(p_copied, t + 2)
                    for g in range(2):
                        mm = split_product(val_ps[:, g, 0:VAL_COLS], [(
                            x1t_hi[:, k, g, :], x1t_lo[:, k, g, :], wv1_hi[:, k, :], wv1_lo[:, k, :])
                            for k in range(HALVES)])
                    mm.then_inc(val_done, 1)
                if exists(t + 2):
                    layer0(t + 2, r + 2, 1)
                if exists(t):
                    pe.wait_ge(z_lo_done, t + 1)
                    if exists(t - 1):
                        pe.wait_ge(x2_done, t)
                    for g in range(2):
                        n = graph(g, NODES)
                        mm = split_product(score_ps[:, g, :], [(
                            z_hi[:, k, n], z_lo[:, k, n], x1t_hi[:, k, g, :], x1t_lo[:, k, g, :])
                            for k in range(HALVES)])
                    mm.then_inc(score_done, 1)

            pe.wait_ge(params0_loaded, 16)
            for m in range(HALVES):
                for k in range(HALVES):
                    mm = nc.tensor.matmul(m0_ps[:, m, :], wqkT[:, k, m * 128:(m + 1) * 128], wqkT[:, 2 + k, :],
                                          start=(k == 0), stop=(k == HALVES - 1))
            mm.then_inc(m0_done, 1)
            pe.wait_ge(params1_loaded, 16)
            for m in range(HALVES):
                for k in range(HALVES):
                    mm = nc.tensor.matmul(at_ps[:, m, :], wk1[:, k, m * 128:(m + 1) * 128], wq1[:, k, :],
                                          start=(k == 0), stop=(k == HALVES - 1))
            mm.then_inc(at_done, 1)
            for n, (w, b) in enumerate(((wq1, bk), (wk1, bq))):
                for m in range(HALVES):
                    for k in range(HALVES):
                        nc.tensor.matmul(bias_ps[:, 2 * n + m:2 * n + m + 1], w[:, k, m * 128:(m + 1) * 128],
                                         b[:, k:k + 1], start=(k == 0), stop=(k == HALVES - 1))
            pe.wait_ge(bq_widened, 1)
            for k in range(HALVES):
                mm = nc.tensor.matmul(bias_ps[:, 4:5], bq_wide[:, k, :], bk[:, k:k + 1], start=(k == 0), stop=(k == HALVES - 1))
            mm.then_inc(bias_done, 1)
            pe.wait_ge(w0_lo_done, 1)
            pe.wait_ge(w1_lo_done, 1)
            pe.wait_ge(ident_ready, 1)
            slots(pe, slot)


def kernel(**inputs):
    import numpy as np
    import concourse.bacc as bacc
    from concourse.bass_utils import run_bass_kernel_spmd

    a = {name: np.asarray(value) for name, value in inputs.items()}

    def rows(w):
        return w.reshape(-1, 128, w.shape[-1]).transpose(1, 0, 2).reshape(128, -1)

    x = a["x"].reshape(PAIRS, 2, NODES, HALVES, 128)
    adjt = a["adj"].reshape(PAIRS, 2, NODES, NODES).transpose(0, 3, 1, 2).reshape(PAIRS, NODES, PAIR_N)
    mask = a["nodemask"].reshape(PAIRS, 2, NODES).transpose(0, 2, 1)
    arrays = {
        "x_pairs": x.transpose(0, 2, 1, 3, 4).reshape(PAIRS, NODES, PAIR_X),
        "xt_pairs": x.transpose(0, 4, 3, 1, 2).reshape(PAIRS, 128, PAIR_X),
        "adjt_pairs": np.concatenate([adjt, mask], axis=2),
        "params0": np.concatenate([rows(a["L0_gnn_Wqk"].T), rows(a["L0_gnn_Wv"])], axis=1),
        "params1": np.concatenate([rows(a["L1_gnn_Wq_w"]), rows(a["L1_gnn_Wk_w"]), rows(a["L1_gnn_Wv_w"].T),
                                   rows(a["L1_gnn_Wq_b"][:, None]), rows(a["L1_gnn_Wk_b"][:, None])], axis=1),
        "value_bias": a["L1_gnn_Wv_b"],
    }
    arrays = {name: np.ascontiguousarray(value) for name, value in arrays.items()}
    nc = bacc.Bacc("TRN2", target_bir_lowering=False, num_devices=1)
    args = [nc.dram_tensor(name, value.shape, F32, kind="ExternalInput").ap() for name, value in arrays.items()]
    out = nc.dram_tensor("out_pairs", (PAIRS, NODES, PAIR_X), F32, kind="ExternalOutput").ap()
    build(nc, *args, out)
    result = run_bass_kernel_spmd(nc, [arrays], core_ids=[0]).results[0]["out_pairs"]
    return result.reshape(PAIRS, NODES, 2, DIM).transpose(0, 2, 1, 3).reshape(GRAPHS, NODES, DIM)
```

```python
from contextlib import ExitStack

import concourse.bass as bass
from concourse import mybir

F32 = mybir.dt.float32
F32R = mybir.dt.float32r
ALU = mybir.AluOpType
ACT = mybir.ActivationFunctionType
AX = mybir.AxisListType

GRAPHS, NODES, DIM = 64, 128, 256
HALVES = DIM // 128
PAIRS = GRAPHS // 2
PAIR_X = 2 * DIM
PAIR_N = 2 * NODES
ADJ_COLS = PAIR_N + 2
VAL_COLS = DIM + 2
EPS = 1e-5
ATT_SCALE = 1.0 / 16.0
P0_COLS = 4 * DIM + HALVES * DIM
P1_COLS = 3 * HALVES * DIM + 2 * HALVES
LOOP_FROM, LOOP_TO, UNROLL = 4, 28, 4
FIRST, LAST = -3, PAIRS + 2


def exists(pair):
    return not isinstance(pair, int) or 0 <= pair < PAIRS


def build(nc, x_pairs, xt_pairs, adjt_pairs, params0, params1, value_bias, out_pairs):
    ctx = ExitStack()
    with ctx:
        def sb(name, shape, dt=F32):
            return ctx.enter_context(nc.sbuf_tensor(name, shape, dt))

        def sem(name):
            return ctx.enter_context(nc.semaphore(name))

        def sems(name, n):
            return [sem(f"{name}{i}") for i in range(n)]

        p0 = sb("p0", [128, P0_COLS])
        p1 = sb("p1", [128, P1_COLS])
        wqkT = p0[:, 0:4 * DIM].rearrange("p (t a) -> p t a", t=4)
        wv0 = p0[:, 4 * DIM:P0_COLS].rearrange("p (t a) -> p t a", t=HALVES)
        wq1, wk1, wv1T = (p1[:, n * 2 * DIM:(n + 1) * 2 * DIM].rearrange("p (t a) -> p t a", t=HALVES)
                          for n in range(3))
        bq = p1[:, 6 * DIM:6 * DIM + 2]
        bk = p1[:, 6 * DIM + 2:6 * DIM + 4]
        bq_wide = sb("bq_wide", [128, HALVES, 128])
        bv_all = sb("bv_all", [128, DIM])
        ident = sb("ident", [128, 128])
        minus_half = sb("minus_half", [128, 4])
        w0_hi = sb("w0_hi", [128, HALVES, 2 * DIM], F32R)
        w0_lo = sb("w0_lo", [128, HALVES, 2 * DIM], F32R)
        at_hi = sb("at_hi", [128, HALVES, DIM], F32R)
        at_lo = sb("at_lo", [128, HALVES, DIM], F32R)
        wv1_hi = sb("wv1_hi", [128, HALVES, VAL_COLS], F32R)
        wv1_lo = sb("wv1_lo", [128, HALVES, VAL_COLS], F32R)
        z_bias = sb("z_bias", [128, HALVES])
        s_bias = sb("s_bias", [128, 1])

        x_raw = [sb(f"x_raw{i}", [128, PAIR_X]) for i in range(4)]
        adjt = [sb(f"adjt{i}", [128, ADJ_COLS]) for i in range(4)]
        xt_raw = [sb(f"xt_raw{i}", [128, PAIR_X]) for i in range(2)]
        xt_hi = [sb(f"xt_hi{i}", [128, HALVES, 2, 128], F32R) for i in range(2)]
        xt_lo = [sb(f"xt_lo{i}", [128, HALVES, 2, 128], F32R) for i in range(2)]
        x_hi = [sb(f"x_hi{i}", [128, PAIR_X], F32R) for i in range(2)]
        x_lo = [sb(f"x_lo{i}", [128, PAIR_X], F32R) for i in range(2)]
        adjm = sb("adjm", [128, PAIR_N])
        adjm_hi = [sb(f"adjm_hi{i}", [128, PAIR_N], F32R) for i in range(2)]
        adjm_lo = [sb(f"adjm_lo{i}", [128, PAIR_N], F32R) for i in range(2)]
        agg = sb("agg", [128, 2, DIM])
        w_col = sb("w_col", [128, 2])
        neg_max = sb("neg_max", [2, 1])
        exp_sum = sb("exp_sum", [2, 1])
        exp_row = sb("exp_row", [2, 128])
        inv_sum = sb("inv_sum", [2, 1])
        inv_diag = sb("inv_diag", [2, 2])
        p_col = sb("p_col", [128, 2])
        x1_sum = [sb(f"x1_sum{i}", [128, PAIR_X]) for i in range(2)]
        x1 = [sb(f"x1_{i}", [128, PAIR_X]) for i in range(2)]
        x1b = [sb(f"x1b{i}", [128, PAIR_X]) for i in range(2)]
        x1t = sb("x1t", [128, HALVES, 2, 128])
        x1t_hi = sb("x1t_hi", [128, HALVES, 2, 128], F32R)
        x1t_lo = sb("x1t_lo", [128, HALVES, 2, 128], F32R)
        z = sb("z", [128, HALVES, PAIR_N])
        val = sb("val", [128, 2, VAL_COLS])
        score_bias = sb("score_bias", [128, 2])
        exp_s = sb("exp_s", [128, PAIR_N])
        edge = sb("edge", [128, PAIR_N])
        den_inv = sb("den_inv", [128, 2])
        x2 = [sb(f"x2_{i}", [128, PAIR_X]) for i in range(4)]
        stats1 = sb("stats1", [128, 2, 6])
        stats2 = sb("stats2", [128, 2, 6])
        mean_var = sb("mean_var", [128, 4, 2])
        var_eps = sb("var_eps", [128, 4])
        rstd = sb("rstd", [128, 4])
        shift = sb("shift", [128, 4])

        ps = ctx.enter_context(nc.psum_tensor("ps", [128, 8, 512], F32))
        x1t_ps = ps[:, 0, :].rearrange("p (t g n) -> p t g n", t=HALVES, g=2)
        z_ps = ps[:, 0, :].rearrange("p (t n) -> p t n", t=HALVES)
        sum_ps = ps[:, 1:3, :]
        score_ps = ps[:, 1:3, 384:512]
        val_ps = ps[:, 3:5, :]
        y_ps = ps[:, 5:7, 0:DIM]
        agg_ps = ps[:, 5:7, DIM:2 * DIM]
        w_row_ps = ps[0:2, 5, 0:NODES]
        p_col_ps = ps[:, 6, 0:2]
        v0_ps = ps[:, 7, :].rearrange("p (g d) -> p g d", g=2)
        m0_ps = ps[:, 5, :].rearrange("p (t a) -> p t a", t=HALVES)
        at_ps = ps[:, 6, :].rearrange("p (t a) -> p t a", t=HALVES)
        bias_ps = ps[:, 7, :]

        params0_loaded, params1_loaded, bv_loaded = sem("params0_loaded"), sem("params1_loaded"), sem("bv_loaded")
        x_loaded, adj_loaded, xt_loaded = sems("x_loaded", 4), sems("adj_loaded", 4), sems("xt_loaded", 2)
        out_stored = sems("out_stored", 4)
        ident_zeroed, ident_ready, consts_ready = sem("ident_zeroed"), sem("ident_ready"), sem("consts_ready")
        bq_widened = sem("bq_widened")
        m0_done, at_done, bias_done = sem("m0_done"), sem("at_done"), sem("bias_done")
        w0_hi_done, w0_lo_done, w1_hi_done, w1_lo_done = sem("w0_hi_done"), sem("w0_lo_done"), sem("w1_hi_done"), sem("w1_lo_done")
        y_done = sems("y_done", 2)
        x1t_done, w_row_done, p_col_done, v0_done = sem("x1t_done"), sem("w_row_done"), sem("p_col_done"), sem("v0_done")
        sum_done, z_done, val_done, score_done = sem("sum_done"), sem("z_done"), sem("val_done"), sem("score_done")
        xt_hi_done, x_hi_done, adjm_hi_done = sem("xt_hi_done"), sem("x_hi_done"), sem("adjm_hi_done")
        agg_copied = sems("agg_copied", 2)
        x1t_copied, row_exp_done, z_copied = sem("x1t_copied"), sem("row_exp_done"), sem("z_copied")
        val_copied, score_exp_done, x1_done, out_done = sem("val_copied"), sem("score_exp_done"), sem("x1_done"), sem("out_done")
        w_done = sems("w_done", 2)
        row_max_done, inv_sum_done, inv_diag_done, p_copied = sem("row_max_done"), sem("inv_sum_done"), sem("inv_diag_done"), sem("p_copied")
        x1_sum_done, stats1_done, x1t_hi_done, x1t_lo_done = sem("x1_sum_done"), sem("stats1_done"), sem("x1t_hi_done"), sem("x1t_lo_done")
        score_bias_done, edge_done, den_inv_done = sem("score_bias_done"), sem("edge_done"), sem("den_inv_done")
        x2_done, stats2_done = sem("x2_done"), sem("stats2_done")
        norms_ready = sem("norms_ready")
        mean_var_done, var_eps_done, shift_done = sem("mean_var_done"), sem("var_eps_done"), sem("shift_done")
        xt_lo_done, x_lo_done, adjm_done, adjm_lo_done = sem("xt_lo_done"), sem("x_lo_done"), sem("adjm_done"), sem("adjm_lo_done")
        x1b_done, rstd_done = sem("x1b_done"), sem("rstd_done")

        def graph(g, width=DIM):
            return slice(g * width, (g + 1) * width)

        def transfers4(u, r):
            return 4 * (u - r % 4) + 16

        def transfers2(u, r):
            return 8 * (u - r % 2) + 16

        def norms(t):
            return t + 2

        def slots(eng, slot):
            for t in range(FIRST, LOOP_FROM):
                slot(t, t)
            with eng.Fori(LOOP_FROM, LOOP_TO - UNROLL + 1, UNROLL) as base:
                for j in range(UNROLL):
                    slot(base + j, LOOP_FROM + j)
            for t in range(LOOP_TO, LAST + 1):
                slot(t, t)

        block = ctx.enter_context(nc.Block())

        @block.sync
        def _(sp):
            def load_x(u, r):
                sp.dma_start(x_raw[r % 4][:, :], x_pairs[u]).then_inc(x_loaded[r % 4], 16)

            def load_xt(u, r):
                sp.dma_start(xt_raw[r % 2][:, :], xt_pairs[u]).then_inc(xt_loaded[r % 2], 16)

            def load_adj(u, r):
                sp.dma_start(adjt[r % 4][:, :], adjt_pairs[u]).then_inc(adj_loaded[r % 4], 16)

            def slot(t, r):
                if exists(t + 3) and exists(t - 1):
                    sp.wait_ge(edge_done, t)
                    load_adj(t + 3, r + 3)
                if exists(t + 4) and exists(t + 2):
                    sp.wait_ge(xt_lo_done, t + 3)
                    load_xt(t + 4, r + 4)
                if exists(t + 4) and exists(t):
                    sp.wait_ge(x1_sum_done, t + 1)
                    load_x(t + 4, r + 4)
                if exists(t - 3):
                    sp.wait_ge(out_done, t - 2)
                    sp.dma_start(out_pairs[t - 3], x2[(r - 3) % 4][:, :]).then_inc(out_stored[(r - 3) % 4], 16)

            sp.dma_start(p0[:, :], params0).then_inc(params0_loaded, 16)
            for u in range(2):
                load_adj(u, u)
                load_xt(u, u)
                load_x(u, u)
                if u == 0:
                    sp.dma_start(p1[:, :], params1).then_inc(params1_loaded, 16)
                    sp.dma_start(bv_all[:, :], value_bias.partition_broadcast(128)).then_inc(bv_loaded, 16)
            for u in range(2, 4):
                load_adj(u, u)
                load_x(u, u)
            for q in out_stored:
                sp.sem_inc(q, 16)
            slots(sp, slot)
            for q in out_stored:
                sp.wait_ge(q, 16 + 16 * PAIRS // 4)

        @block.gpsimd
        def _(pool):
            def slot(t, r):
                if exists(t + 3):
                    pool.wait_ge(xt_hi_done, t + 4)
                    nc.gpsimd.tensor_tensor(
                        xt_lo[(r + 3) % 2][:, :, :, :].rearrange("p t g n -> p (t g n)"), xt_raw[(r + 3) % 2][:, :],
                        xt_hi[(r + 3) % 2][:, :, :, :].rearrange("p t g n -> p (t g n)").bitcast(F32), ALU.subtract)\
                        .then_inc(xt_lo_done, 1)
                if exists(t + 3):
                    pool.wait_ge(adj_loaded[(r + 3) % 4], transfers4(t + 3, r + 3))
                    if exists(t + 2):
                        pool.wait_ge(adjm_lo_done, t + 3)
                    a = adjt[(r + 3) % 4]
                    nc.gpsimd.tensor_tensor(
                        adjm[:, :].rearrange("p (g n) -> p g n", g=2),
                        a[:, 0:PAIR_N].rearrange("p (g n) -> p g n", g=2),
                        a[:, PAIR_N:ADJ_COLS].unsqueeze(2).broadcast_to([128, 2, NODES]), ALU.mult)\
                        .then_inc(adjm_done, 1)
                if exists(t + 1) or exists(t - 2):
                    pool.wait_ge(var_eps_done, norms(t))
                    if exists(t):
                        pool.wait_ge(x1_done, t + 1)
                    if exists(t - 3):
                        pool.wait_ge(out_done, t - 2)
                    nc.gpsimd.tensor_tensor(rstd[:, :], var_eps[:, :], minus_half[:, :], ALU.pow).then_inc(rstd_done, 1)
                if exists(t + 3):
                    pool.wait_ge(x_hi_done, t + 4)
                    nc.gpsimd.tensor_tensor(x_lo[(r + 3) % 2][:, :], x_raw[(r + 3) % 4][:, :],
                                            x_hi[(r + 3) % 2][:, :].bitcast(F32), ALU.subtract).then_inc(x_lo_done, 1)
                    pool.wait_ge(adjm_hi_done, t + 4)
                    nc.gpsimd.tensor_tensor(adjm_lo[(r + 3) % 2][:, :], adjm[:, :],
                                            adjm_hi[(r + 3) % 2][:, :].bitcast(F32), ALU.subtract).then_inc(adjm_lo_done, 1)
                if exists(t):
                    pool.wait_ge(x1_done, t + 1)
                    if isinstance(t, int) and t == 0:
                        pool.wait_ge(bv_loaded, 16)
                    nc.gpsimd.tensor_tensor(
                        x1b[r % 2][:, :].rearrange("p (g d) -> p g d", g=2),
                        x1[r % 2][:, :].rearrange("p (g d) -> p g d", g=2),
                        bv_all[:, :].unsqueeze(1).broadcast_to([128, 2, DIM]), ALU.add).then_inc(x1b_done, 1)

            nc.gpsimd.memset(ident[:, :], 0.0).then_inc(ident_zeroed, 1)
            nc.gpsimd.memset(minus_half[:, :], -0.5)
            nc.gpsimd.memset(wv1_hi[:, :, DIM:VAL_COLS].bitcast(F32), 0.0)
            nc.gpsimd.memset(wv1_lo[:, :, DIM:VAL_COLS].bitcast(F32), 0.0)
            nc.gpsimd.memset(val[:, :, DIM:DIM + 1], 1.0)
            nc.gpsimd.memset(val[:, :, DIM + 1:VAL_COLS], 0.0).then_inc(consts_ready, 1)
            pool.wait_ge(ident_zeroed, 1)
            nc.gpsimd.affine_select(out=ident[:, :], in_=ident[:, :], compare_op=ALU.not_equal, fill=1.0, base=0,
                                    pattern=[[-1, 128]], channel_multiplier=1).then_inc(ident_ready, 1)
            pool.wait_ge(consts_ready, 1)
            slots(pool, slot)

        @block.scalar
        def _(act):
            def copy_agg(u, g):
                act.wait_ge(y_done[g], u + 1)
                if exists(u - 1):
                    act.wait_ge(w_done[g], u)
                nc.scalar.copy(agg[:, g, :], agg_ps[:, g, :]).then_inc(agg_copied[g], 1)

            def norm(out, in_, first, done):
                for g in range(2):
                    n = first + g
                    last = nc.scalar.activation(out[:, graph(g)], in_[:, graph(g)], ACT.Identity,
                                                bias=shift[:, n:n + 1], scale=rstd[:, n:n + 1])
                last.then_inc(done, 1)

            def slot(t, r):
                if exists(t - 1):
                    act.wait_ge(score_done, t)
                    act.wait_ge(score_bias_done, t)
                    if exists(t - 2):
                        act.wait_ge(edge_done, t - 1)
                    for g in range(2):
                        last = nc.scalar.activation(exp_s[:, graph(g, NODES)], score_ps[:, g, :], ACT.Exp,
                                                    bias=score_bias[:, g:g + 1])
                    last.then_inc(score_exp_done, 1)
                if exists(t):
                    act.wait_ge(x1t_done, t + 1)
                    nc.scalar.copy(x1t[:, :, :, :], x1t_ps).then_inc(x1t_copied, 1)
                if exists(t + 3):
                    act.wait_ge(xt_loaded[(r + 3) % 2], transfers2(t + 3, r + 3))
                    if exists(t + 1):
                        act.wait_ge(v0_done, t + 2)
                    nc.scalar.copy(xt_hi[(r + 3) % 2][:, :, :, :].rearrange("p t g n -> p (t g n)"),
                                   xt_raw[(r + 3) % 2][:, :]).then_inc(xt_hi_done, 1)
                if exists(t + 2):
                    copy_agg(t + 2, 0)
                if exists(t + 3):
                    act.wait_ge(x_loaded[(r + 3) % 4], transfers4(t + 3, r + 3))
                    nc.scalar.copy(x_hi[(r + 3) % 2][:, :], x_raw[(r + 3) % 4][:, :]).then_inc(x_hi_done, 1)
                if exists(t + 2):
                    copy_agg(t + 2, 1)
                if exists(t - 3):
                    act.wait_ge(shift_done, norms(t) - 1)
                    norm(x2[(r - 3) % 4], x2[(r - 3) % 4], 2, out_done)
                if exists(t + 3):
                    act.wait_ge(adjm_done, t + 4)
                    nc.scalar.copy(adjm_hi[(r + 3) % 2][:, :], adjm[:, :]).then_inc(adjm_hi_done, 1)
                if exists(t):
                    act.wait_ge(z_done, t + 1)
                    for m in range(HALVES):
                        last = nc.scalar.activation(z[:, m, :], z_ps[:, m, :], ACT.Identity, bias=z_bias[:, m:m + 1])
                    last.then_inc(z_copied, 1)
                if exists(t + 2):
                    act.wait_ge(row_max_done, t + 3)
                    nc.scalar.activation(exp_row[:, :], w_row_ps, ACT.Exp, bias=neg_max[:, 0:1],
                                         accum_out=exp_sum[:, 0:1]).then_inc(row_exp_done, 1)
                if exists(t + 1):
                    act.wait_ge(shift_done, norms(t))
                    if exists(t - 1):
                        act.wait_ge(x1b_done, t)
                    norm(x1[(r + 1) % 2], x1_sum[(r + 1) % 2], 0, x1_done)
                if exists(t):
                    act.wait_ge(val_done, t + 1)
                    nc.scalar.copy(val[:, :, 0:DIM], val_ps[:, :, 0:DIM]).then_inc(val_copied, 1)

            act.wait_ge(params0_loaded, 16)
            nc.scalar.copy(w0_hi[:, :, DIM:2 * DIM], wv0)
            act.wait_ge(m0_done, 1)
            nc.scalar.activation(w0_hi[:, :, 0:DIM], m0_ps, ACT.Copy, scale=ATT_SCALE).then_inc(w0_hi_done, 1)
            act.wait_ge(params1_loaded, 16)
            act.wait_ge(consts_ready, 1)
            nc.scalar.copy(wv1_hi[:, :, 0:DIM], wv1T)
            act.wait_ge(at_done, 1)
            nc.scalar.copy(at_hi[:, :, :], at_ps)
            act.wait_ge(bias_done, 1)
            nc.scalar.copy(wv1_hi[:, :, DIM], bias_ps[:, 2:4]).then_inc(w1_hi_done, 1)
            slots(act, slot)

        @block.vector
        def _(dve):
            def weight(u, r, g):
                dve.wait_ge(agg_copied[g], u + 1)
                if exists(u - 1):
                    dve.wait_ge(w_row_done, u)
                nc.vector.tensor_tensor_reduce(agg[:, g, :], y_ps[:, g, :], agg[:, g, :],
                                               adjt[r % 4][:, PAIR_N + g:PAIR_N + g + 1], 0.0, ALU.mult, ALU.add,
                                               w_col[:, g:g + 1]).then_inc(w_done[g], 1)

            def slot(t, r):
                if exists(t + 1):
                    dve.wait_ge(v0_done, t + 2)
                    if exists(t - 1):
                        dve.wait_ge(x1_done, t)
                    dve.wait_ge(p_copied, t + 2)
                    for g in range(2):
                        last = nc.vector.scalar_tensor_tensor(
                            out=x1_sum[(r + 1) % 2][:, graph(g)], in0=v0_ps[:, g, :], scalar=p_col[:, g:g + 1],
                            in1=x_raw[(r + 1) % 4][:, graph(g)], op0=ALU.mult, op1=ALU.add)
                    last.then_inc(x1_sum_done, 1)
                if exists(t - 1):
                    dve.wait_ge(score_exp_done, t)
                    if exists(t - 2):
                        dve.wait_ge(sum_done, t - 1)
                    nc.vector.tensor_tensor(edge[:, :], exp_s[:, :], adjt[(r - 1) % 4][:, 0:PAIR_N], ALU.mult)\
                        .then_inc(edge_done, 1)
                if exists(t):
                    dve.wait_ge(x1t_copied, t + 1)
                    nc.vector.tensor_copy(x1t_hi[:, :, :, :], x1t[:, :, :, :]).then_inc(x1t_hi_done, 1)
                if exists(t):
                    dve.wait_ge(x1t_hi_done, t + 1)
                    nc.vector.tensor_tensor(x1t_lo[:, :, :, :], x1t[:, :, :, :], x1t_hi[:, :, :, :].bitcast(F32),
                                            ALU.subtract).then_inc(x1t_lo_done, 1)
                if exists(t + 1):
                    dve.wait_ge(x1_sum_done, t + 2)
                    for g in range(2):
                        last = nc.vector.bn_stats(stats1[:, g, :], x1_sum[(r + 1) % 2][:, graph(g)])
                    last.then_inc(stats1_done, 1)
                if exists(t + 1) or exists(t - 2):
                    dve.wait_ge(norms_ready, 1)
                    if exists(t):
                        dve.wait_ge(shift_done, norms(t) - 1)
                    if exists(t + 1):
                        dve.wait_ge(stats1_done, t + 2)
                    if exists(t - 2):
                        dve.wait_ge(stats2_done, t - 1)
                    for g in range(2):
                        if exists(t + 1):
                            last = nc.vector.bn_aggr(mean_var[:, g, :], stats1[:, g, :])
                        if exists(t - 2):
                            last = nc.vector.bn_aggr(mean_var[:, 2 + g, :], stats2[:, g, :])
                    last.then_inc(mean_var_done, 1)
                    dve.wait_ge(mean_var_done, norms(t))
                    nc.vector.tensor_scalar(var_eps[:, :], mean_var[:, :, 1], EPS, None, ALU.add).then_inc(var_eps_done, 1)
                if exists(t + 2):
                    for g in range(2):
                        weight(t + 2, r + 2, g)
                if exists(t - 1):
                    dve.wait_ge(sum_done, t)
                    nc.vector.reciprocal(den_inv[:, :], sum_ps[:, :, DIM]).then_inc(den_inv_done, 1)
                    dve.wait_ge(x1b_done, t)
                    dve.wait_ge(out_stored[(r - 1) % 4], transfers4(t - 1, r - 1))
                    dve.wait_ge(den_inv_done, t)
                    for g in range(2):
                        last = nc.vector.scalar_tensor_tensor(
                            out=x2[(r - 1) % 4][:, graph(g)], in0=sum_ps[:, g, 0:DIM], scalar=den_inv[:, g:g + 1],
                            in1=x1b[(r - 1) % 2][:, graph(g)], op0=ALU.mult, op1=ALU.add)
                    last.then_inc(x2_done, 1)
                if exists(t + 1) or exists(t - 2):
                    dve.wait_ge(rstd_done, norms(t))
                    nc.vector.scalar_tensor_tensor(out=shift[:, :], in0=mean_var[:, :, 0], scalar=-1.0, in1=rstd[:, :],
                                                   op0=ALU.mult, op1=ALU.mult).then_inc(shift_done, 1)
                if exists(t + 2):
                    dve.wait_ge(w_row_done, t + 3)
                    nc.vector.tensor_reduce(neg_max[:, :], w_row_ps, AX.X, ALU.max, negate=True).then_inc(row_max_done, 1)
                if exists(t + 2):
                    dve.wait_ge(row_exp_done, t + 3)
                    nc.vector.reciprocal(inv_sum[:, :], exp_sum[:, :]).then_inc(inv_sum_done, 1)
                    dve.wait_ge(inv_sum_done, t + 3)
                    nc.vector.tensor_scalar(inv_diag[:, :], ident[0:2, 0:2], inv_sum[:, 0:1], None, ALU.mult)\
                        .then_inc(inv_diag_done, 1)
                if exists(t - 1):
                    dve.wait_ge(x2_done, t)
                    for g in range(2):
                        last = nc.vector.bn_stats(stats2[:, g, :], x2[(r - 1) % 4][:, graph(g)])
                    last.then_inc(stats2_done, 1)
                if exists(t + 2):
                    dve.wait_ge(p_col_done, t + 3)
                    if exists(t + 1):
                        dve.wait_ge(x1_sum_done, t + 2)
                    nc.vector.tensor_copy(p_col[:, :], p_col_ps).then_inc(p_copied, 1)
                if exists(t):
                    dve.wait_ge(val_copied, t + 1)
                    nc.vector.tensor_scalar(score_bias[:, :], val_ps[:, :, DIM], s_bias[:, 0:1], None, ALU.add)\
                        .then_inc(score_bias_done, 1)

            nc.vector.memset(mean_var[:, :, :], 1.0).then_inc(norms_ready, 1)
            dve.wait_ge(w0_hi_done, 1)
            nc.vector.tensor_tensor(w0_lo[:, :, DIM:2 * DIM], wv0, w0_hi[:, :, DIM:2 * DIM].bitcast(F32), ALU.subtract)
            nc.vector.scalar_tensor_tensor(
                out=w0_lo[:, :, 0:DIM], in0=m0_ps, scalar=ATT_SCALE,
                in1=w0_hi[:, :, 0:DIM].bitcast(F32), op0=ALU.mult, op1=ALU.subtract).then_inc(w0_lo_done, 1)
            dve.wait_ge(params1_loaded, 16)
            nc.vector.tensor_copy(bq_wide[:, :, :], bq.unsqueeze(2).broadcast_to([128, HALVES, 128])).then_inc(bq_widened, 1)
            dve.wait_ge(w1_hi_done, 1)
            dve.wait_ge(norms_ready, 1)
            nc.vector.tensor_tensor(wv1_lo[:, :, 0:DIM], wv1T, wv1_hi[:, :, 0:DIM].bitcast(F32), ALU.subtract)
            nc.vector.tensor_tensor(at_lo[:, :, :], at_ps, at_hi[:, :, :].bitcast(F32), ALU.subtract)
            nc.vector.tensor_tensor(wv1_lo[:, :, DIM], bias_ps[:, 2:4], wv1_hi[:, :, DIM].bitcast(F32), ALU.subtract)
            nc.vector.tensor_copy(z_bias[:, :], bias_ps[:, 0:2])
            nc.vector.tensor_copy(s_bias[:, :], bias_ps[:, 4:5]).then_inc(w1_lo_done, 1)
            dve.wait_ge(w1_lo_done, 1)
            dve.wait_ge(ident_ready, 1)
            slots(dve, slot)

        @block.tensor
        def _(pe):
            def split_product(out, parts):
                for n, (s_hi, s_lo, m_hi, m_lo) in enumerate(parts):
                    nc.tensor.matmul(out, s_hi, m_hi, start=(n == 0), stop=False)
                    nc.tensor.matmul(out, s_hi, m_lo, start=False, stop=False)
                    mm = nc.tensor.matmul(out, s_lo, m_hi, start=False, stop=(n == len(parts) - 1))
                return mm

            def layer0(u, r, g):
                pe.wait_ge(adjm_lo_done, u + 1)
                if exists(u - 1):
                    pe.wait_ge(w_done[g], u)
                    pe.wait_ge(p_copied, u)
                n = graph(g, NODES)
                split_product(agg_ps[:, g, :], [(adjm_hi[r % 2][:, n], adjm_lo[r % 2][:, n],
                                                 x_hi[r % 2][:, graph(g)], x_lo[r % 2][:, graph(g)])])
                split_product(y_ps[:, g, :], [(xt_hi[r % 2][:, k, g, :], xt_lo[r % 2][:, k, g, :],
                                               w0_hi[:, k, 0:DIM], w0_lo[:, k, 0:DIM]) for k in range(HALVES)])\
                    .then_inc(y_done[g], 1)

            def slot(t, r):
                if exists(t):
                    pe.wait_ge(x1_done, t + 1)
                    if exists(t - 1):
                        pe.wait_ge(z_copied, t)
                    for g in range(2):
                        for k in range(HALVES):
                            c = g * DIM + k * 128
                            mm = nc.tensor.transpose(x1t_ps[:, k, g, :], x1[r % 2][:, c:c + 128], ident[:, :])
                    mm.then_inc(x1t_done, 1)
                if exists(t + 2):
                    for g in range(2):
                        layer0(t + 2, r + 2, g)
                if exists(t - 1):
                    pe.wait_ge(edge_done, t)
                    pe.wait_ge(val_copied, t)
                    for g in range(2):
                        mm = nc.tensor.matmul(sum_ps[:, g, 0:VAL_COLS], edge[:, graph(g, NODES)], val[:, g, :],
                                              start=True, stop=True)
                    mm.then_inc(sum_done, 1)
                if exists(t):
                    pe.wait_ge(x1t_lo_done, t + 1)
                    for m in range(HALVES):
                        c = slice(m * 128, (m + 1) * 128)
                        mm = split_product(z_ps[:, m, :], [(
                            at_hi[:, k, c], at_lo[:, k, c], x1t_hi[:, k, :, :].rearrange("p g n -> p (g n)"),
                            x1t_lo[:, k, :, :].rearrange("p g n -> p (g n)")) for k in range(HALVES)])
                    mm.then_inc(z_done, 1)
                    for g in range(2):
                        mm = split_product(val_ps[:, g, 0:VAL_COLS], [(
                            x1t_hi[:, k, g, :], x1t_lo[:, k, g, :], wv1_hi[:, k, :], wv1_lo[:, k, :])
                            for k in range(HALVES)])
                    mm.then_inc(val_done, 1)
                if exists(t + 2):
                    for g in range(2):
                        pe.wait_ge(w_done[g], t + 3)
                    nc.tensor.transpose(w_row_ps, w_col[:, :], ident[:, :]).then_inc(w_row_done, 1)
                    if exists(t + 1):
                        pe.wait_ge(x1_sum_done, t + 2)
                    for g in range(2):
                        mm = split_product(v0_ps[:, g, :], [(
                            xt_hi[r % 2][:, k, g, :], xt_lo[r % 2][:, k, g, :],
                            w0_hi[:, k, DIM:2 * DIM], w0_lo[:, k, DIM:2 * DIM]) for k in range(HALVES)])
                    mm.then_inc(v0_done, 1)
                for g in range(2):
                    if exists(t):
                        if g == 0:
                            pe.wait_ge(z_copied, t + 1)
                            if exists(t - 1):
                                pe.wait_ge(x2_done, t)
                        for k in range(HALVES):
                            mm = nc.tensor.matmul(score_ps[:, g, :], z[:, k, graph(g, NODES)], x1t[:, k, g, :],
                                                  start=(k == 0), stop=(k == HALVES - 1))
                        if g == 1:
                            mm.then_inc(score_done, 1)
                    if g == 0 and exists(t + 2):
                        pe.wait_ge(inv_diag_done, t + 3)
                        nc.tensor.matmul(p_col_ps, exp_row[:, :], inv_diag[:, :], start=True, stop=True)\
                            .then_inc(p_col_done, 1)

            pe.wait_ge(params0_loaded, 16)
            for m in range(HALVES):
                for k in range(HALVES):
                    mm = nc.tensor.matmul(m0_ps[:, m, :], wqkT[:, k, m * 128:(m + 1) * 128], wqkT[:, 2 + k, :],
                                          start=(k == 0), stop=(k == HALVES - 1))
            mm.then_inc(m0_done, 1)
            pe.wait_ge(params1_loaded, 16)
            for m in range(HALVES):
                for k in range(HALVES):
                    mm = nc.tensor.matmul(at_ps[:, m, :], wk1[:, k, m * 128:(m + 1) * 128], wq1[:, k, :],
                                          start=(k == 0), stop=(k == HALVES - 1))
            mm.then_inc(at_done, 1)
            for n, (w, b) in enumerate(((wq1, bk), (wk1, bq))):
                for m in range(HALVES):
                    for k in range(HALVES):
                        nc.tensor.matmul(bias_ps[:, 2 * n + m:2 * n + m + 1], w[:, k, m * 128:(m + 1) * 128],
                                         b[:, k:k + 1], start=(k == 0), stop=(k == HALVES - 1))
            pe.wait_ge(bq_widened, 1)
            for k in range(HALVES):
                mm = nc.tensor.matmul(bias_ps[:, 4:5], bq_wide[:, k, :], bk[:, k:k + 1], start=(k == 0), stop=(k == HALVES - 1))
            mm.then_inc(bias_done, 1)
            pe.wait_ge(w0_lo_done, 1)
            pe.wait_ge(w1_lo_done, 1)
            pe.wait_ge(ident_ready, 1)
            slots(pe, slot)


def kernel(**inputs):
    import numpy as np
    import concourse.bacc as bacc
    from concourse.bass_utils import run_bass_kernel_spmd

    a = {name: np.asarray(value) for name, value in inputs.items()}

    def rows(w):
        return w.reshape(-1, 128, w.shape[-1]).transpose(1, 0, 2).reshape(128, -1)

    x = a["x"].reshape(PAIRS, 2, NODES, HALVES, 128)
    adjt = a["adj"].reshape(PAIRS, 2, NODES, NODES).transpose(0, 3, 1, 2).reshape(PAIRS, NODES, PAIR_N)
    mask = a["nodemask"].reshape(PAIRS, 2, NODES).transpose(0, 2, 1)
    arrays = {
        "x_pairs": x.transpose(0, 2, 1, 3, 4).reshape(PAIRS, NODES, PAIR_X),
        "xt_pairs": x.transpose(0, 4, 3, 1, 2).reshape(PAIRS, 128, PAIR_X),
        "adjt_pairs": np.concatenate([adjt, mask], axis=2),
        "params0": np.concatenate([rows(a["L0_gnn_Wqk"].T), rows(a["L0_gnn_Wv"])], axis=1),
        "params1": np.concatenate([rows(a["L1_gnn_Wq_w"]), rows(a["L1_gnn_Wk_w"]), rows(a["L1_gnn_Wv_w"].T),
                                   rows(a["L1_gnn_Wq_b"][:, None]), rows(a["L1_gnn_Wk_b"][:, None])], axis=1),
        "value_bias": a["L1_gnn_Wv_b"],
    }
    arrays = {name: np.ascontiguousarray(value) for name, value in arrays.items()}
    nc = bacc.Bacc("TRN2", target_bir_lowering=False, num_devices=1)
    args = [nc.dram_tensor(name, value.shape, F32, kind="ExternalInput").ap() for name, value in arrays.items()]
    out = nc.dram_tensor("out_pairs", (PAIRS, NODES, PAIR_X), F32, kind="ExternalOutput").ap()
    build(nc, *args, out)
    result = run_bass_kernel_spmd(nc, [arrays], core_ids=[0]).results[0]["out_pairs"]
    return result.reshape(PAIRS, NODES, 2, DIM).transpose(0, 2, 1, 3).reshape(GRAPHS, NODES, DIM)
```

```python
from contextlib import ExitStack

import concourse.bass as bass
from concourse import mybir

F32 = mybir.dt.float32
F32R = mybir.dt.float32r
ALU = mybir.AluOpType
ACT = mybir.ActivationFunctionType
AX = mybir.AxisListType

GRAPHS, NODES, DIM = 64, 128, 256
HALVES = DIM // 128
PAIRS = GRAPHS // 2
PAIR_X = 2 * DIM
PAIR_N = 2 * NODES
ADJ_COLS = PAIR_N + 2
VAL_COLS = DIM + 2
EPS = 1e-5
ATT_SCALE = 1.0 / 16.0
P0_COLS = 4 * DIM + HALVES * DIM
P1_COLS = 3 * HALVES * DIM + 2 * HALVES
WARM_UP = 5
LOOP_FROM, LOOP_TO, UNROLL = 4, 28, 4
FIRST, LAST = -2, PAIRS + 2


def exists(pair):
    return not isinstance(pair, int) or 0 <= pair < PAIRS


def build(nc, x_pairs, xt_pairs, adjt_pairs, params0, params1, value_bias, out_pairs):
    ctx = ExitStack()
    with ctx:
        def sb(name, shape, dt=F32):
            return ctx.enter_context(nc.sbuf_tensor(name, shape, dt))

        def sem(name):
            return ctx.enter_context(nc.semaphore(name))

        def sems(name, n):
            return [sem(f"{name}{i}") for i in range(n)]

        p0 = sb("p0", [128, P0_COLS])
        p1 = sb("p1", [128, P1_COLS])
        wqkT = p0[:, 0:4 * DIM].rearrange("p (t a) -> p t a", t=4)
        wv0 = p0[:, 4 * DIM:P0_COLS].rearrange("p (t a) -> p t a", t=HALVES)
        wq1, wk1, wv1T = (p1[:, n * 2 * DIM:(n + 1) * 2 * DIM].rearrange("p (t a) -> p t a", t=HALVES)
                          for n in range(3))
        bq = p1[:, 6 * DIM:6 * DIM + 2]
        bk = p1[:, 6 * DIM + 2:6 * DIM + 4]
        bq_wide = sb("bq_wide", [128, HALVES, 128])
        bv_all = sb("bv_all", [128, DIM])
        ident = sb("ident", [128, 128])
        minus_half = sb("minus_half", [128, 4])
        w0_hi = sb("w0_hi", [128, HALVES, 2 * DIM], F32R)
        w0_lo = sb("w0_lo", [128, HALVES, 2 * DIM], F32R)
        at_hi = sb("at_hi", [128, HALVES, DIM], F32R)
        at_lo = sb("at_lo", [128, HALVES, DIM], F32R)
        wv1_hi = sb("wv1_hi", [128, HALVES, VAL_COLS], F32R)
        wv1_lo = sb("wv1_lo", [128, HALVES, VAL_COLS], F32R)
        z_bias = sb("z_bias", [128, HALVES])
        s_bias = sb("s_bias", [128, 1])

        x_raw = [sb(f"x_raw{i}", [128, PAIR_X]) for i in range(4)]
        adjt = [sb(f"adjt{i}", [128, ADJ_COLS]) for i in range(4)]
        xt_raw = [sb(f"xt_raw{i}", [128, PAIR_X]) for i in range(2)]
        xt_hi = [sb(f"xt_hi{i}", [128, HALVES, 2, 128], F32R) for i in range(2)]
        xt_lo = [sb(f"xt_lo{i}", [128, HALVES, 2, 128], F32R) for i in range(2)]
        x_hi = [sb(f"x_hi{i}", [128, PAIR_X], F32R) for i in range(2)]
        x_lo = [sb(f"x_lo{i}", [128, PAIR_X], F32R) for i in range(2)]
        adjm = sb("adjm", [128, PAIR_N])
        adjm_hi = [sb(f"adjm_hi{i}", [128, PAIR_N], F32R) for i in range(2)]
        adjm_lo = [sb(f"adjm_lo{i}", [128, PAIR_N], F32R) for i in range(2)]
        agg = sb("agg", [128, 2, DIM])
        w_col = sb("w_col", [128, 2])
        neg_max = sb("neg_max", [2, 1])
        exp_sum = sb("exp_sum", [2, 1])
        exp_row = sb("exp_row", [2, 128])
        inv_sum = sb("inv_sum", [2, 1])
        inv_diag = sb("inv_diag", [2, 2])
        p_col = sb("p_col", [128, 2])
        x1_sum = [sb(f"x1_sum{i}", [128, PAIR_X]) for i in range(2)]
        x1 = [sb(f"x1_{i}", [128, PAIR_X]) for i in range(2)]
        x1b = [sb(f"x1b{i}", [128, PAIR_X]) for i in range(2)]
        x1t = sb("x1t", [128, HALVES, 2, 128])
        x1t_hi = sb("x1t_hi", [128, HALVES, 2, 128], F32R)
        x1t_lo = sb("x1t_lo", [128, HALVES, 2, 128], F32R)
        z = sb("z", [128, HALVES, PAIR_N])
        val = sb("val", [128, 2, VAL_COLS])
        score_bias = sb("score_bias", [128, 2])
        exp_s = sb("exp_s", [128, PAIR_N])
        edge = sb("edge", [128, PAIR_N])
        den_inv = sb("den_inv", [128, 2])
        x2 = [sb(f"x2_{i}", [128, PAIR_X]) for i in range(4)]
        stats1 = sb("stats1", [128, 2, 6])
        stats2 = sb("stats2", [128, 2, 6])
        mean_var = sb("mean_var", [128, 4, 2])
        var_eps = sb("var_eps", [128, 4])
        rstd = sb("rstd", [128, 4])
        shift = sb("shift", [128, 4])

        ps = ctx.enter_context(nc.psum_tensor("ps", [128, 8, 512], F32))
        x1t_ps = ps[:, 0, :].rearrange("p (t g n) -> p t g n", t=HALVES, g=2)
        z_ps = ps[:, 0, :].rearrange("p (t n) -> p t n", t=HALVES)
        sum_ps = ps[:, 1:3, :]
        score_ps = ps[:, 1:3, 384:512]
        val_ps = ps[:, 3:5, :]
        y_ps = ps[:, 5:7, 0:DIM]
        agg_ps = ps[:, 5:7, DIM:2 * DIM]
        w_row_ps = ps[0:2, 5, 0:NODES]
        p_col_ps = ps[:, 6, 0:2]
        v0_ps = ps[:, 7, :].rearrange("p (g d) -> p g d", g=2)
        m0_ps = ps[:, 7, :].rearrange("p (t a) -> p t a", t=HALVES)
        at_ps = ps[:, 3, :].rearrange("p (t a) -> p t a", t=HALVES)
        bias_ps = ps[:, 4, :]

        wqk_loaded, wv0_loaded, params1_loaded, bv_loaded = sem("wqk_loaded"), sem("wv0_loaded"), sem("params1_loaded"), sem("bv_loaded")
        x_loaded, adj_loaded, xt_loaded = sems("x_loaded", 4), sems("adj_loaded", 4), sems("xt_loaded", 2)
        out_stored = sems("out_stored", 4)
        ident_zeroed, ident_ready, consts_ready = sem("ident_zeroed"), sem("ident_ready"), sem("consts_ready")
        bq_widened = sem("bq_widened")
        m0_done, at_done, bias_done = sem("m0_done"), sem("at_done"), sem("bias_done")
        m0_hi_done, m0_lo_done, wv0_hi_done, wv0_lo_done = sem("m0_hi_done"), sem("m0_lo_done"), sem("wv0_hi_done"), sem("wv0_lo_done")
        wv1_hi_done, at_hi_done, bias_hi_done, w1_lo_done = sem("wv1_hi_done"), sem("at_hi_done"), sem("bias_hi_done"), sem("w1_lo_done")
        y_done = sems("y_done", 2)
        x1t_done, w_row_done, p_col_done, v0_done = sem("x1t_done"), sem("w_row_done"), sem("p_col_done"), sem("v0_done")
        sum_done, z_done, val_done, score_done = sem("sum_done"), sem("z_done"), sem("val_done"), sem("score_done")
        xt_hi_done, x_hi_done, adjm_hi_done = sem("xt_hi_done"), sem("x_hi_done"), sem("adjm_hi_done")
        agg_copied = sems("agg_copied", 2)
        x1t_copied, row_exp_done, z_copied = sem("x1t_copied"), sem("row_exp_done"), sem("z_copied")
        val_copied, score_exp_done, x1_done, out_done = sem("val_copied"), sem("score_exp_done"), sem("x1_done"), sem("out_done")
        w_done = sems("w_done", 2)
        row_max_done, inv_sum_done, inv_diag_done, p_copied = sem("row_max_done"), sem("inv_sum_done"), sem("inv_diag_done"), sem("p_copied")
        x1_sum_done, stats1_done, x1t_hi_done, x1t_lo_done = sem("x1_sum_done"), sem("stats1_done"), sem("x1t_hi_done"), sem("x1t_lo_done")
        score_bias_done, edge_done, den_inv_done = sem("score_bias_done"), sem("edge_done"), sem("den_inv_done")
        x2_done, stats2_done = sem("x2_done"), sem("stats2_done")
        norms_ready = sem("norms_ready")
        mean_var_done, var_eps_done, shift_done = sem("mean_var_done"), sem("var_eps_done"), sem("shift_done")
        first_xt_lo_done, first_x_lo_done = sem("first_xt_lo_done"), sem("first_x_lo_done")
        xt_lo_done, adjm_done, adjm_lo_done = sem("xt_lo_done"), sem("adjm_done"), sem("adjm_lo_done")
        x1b_done, rstd_done = sem("x1b_done"), sem("rstd_done")

        def graph(g, width=DIM):
            return slice(g * width, (g + 1) * width)

        def transfers4(u, r):
            return 4 * (u - r % 4) + 16

        def transfers2(u, r):
            return 8 * (u - r % 2) + 16

        def norms(t):
            return t + 2

        def slots(eng, slot):
            for t in range(FIRST, LOOP_FROM):
                slot(t, t)
            with eng.Fori(LOOP_FROM, LOOP_TO - UNROLL + 1, UNROLL) as base:
                for j in range(UNROLL):
                    slot(base + j, LOOP_FROM + j)
            for t in range(LOOP_TO, LAST + 1):
                slot(t, t)

        block = ctx.enter_context(nc.Block())

        @block.sync
        def _(sp):
            def load_x(u, r):
                sp.dma_start(x_raw[r % 4][:, :], x_pairs[u]).then_inc(x_loaded[r % 4], 16)

            def load_xt(u, r):
                sp.dma_start(xt_raw[r % 2][:, :], xt_pairs[u]).then_inc(xt_loaded[r % 2], 16)

            def load_adj(u, r):
                sp.dma_start(adjt[r % 4][:, :], adjt_pairs[u]).then_inc(adj_loaded[r % 4], 16)

            def slot(t, r):
                if exists(t + 3) and exists(t - 1):
                    sp.wait_ge(edge_done, t)
                    load_adj(t + 3, r + 3)
                if exists(t + 4) and exists(t + 2):
                    if r + 2 == 0:
                        sp.wait_ge(first_xt_lo_done, 1)
                    else:
                        sp.wait_ge(xt_lo_done, t + 2)
                    load_xt(t + 4, r + 4)
                if exists(t + 4) and exists(t):
                    sp.wait_ge(x1_sum_done, t + 1)
                    load_x(t + 4, r + 4)
                if exists(t - 3):
                    sp.wait_ge(out_done, t - 2)
                    sp.dma_start(out_pairs[t - 3], x2[(r - 3) % 4][:, :]).then_inc(out_stored[(r - 3) % 4], 16)

            sp.dma_start(p0[:, 0:4 * DIM], params0[:, 0:4 * DIM]).then_inc(wqk_loaded, 16)
            for u in range(2):
                load_adj(u, u)
                load_xt(u, u)
                load_x(u, u)
                if u == 0:
                    sp.dma_start(p0[:, 4 * DIM:P0_COLS], params0[:, 4 * DIM:P0_COLS]).then_inc(wv0_loaded, 16)
                    sp.dma_start(p1[:, :], params1).then_inc(params1_loaded, 16)
                    sp.dma_start(bv_all[:, :], value_bias.partition_broadcast(128)).then_inc(bv_loaded, 16)
            for u in range(2, 4):
                load_adj(u, u)
                load_x(u, u)
            for q in out_stored:
                sp.sem_inc(q, 16)
            slots(sp, slot)
            for q in out_stored:
                sp.wait_ge(q, 16 + 16 * PAIRS // 4)

        @block.gpsimd
        def _(pool):
            def mask_adj(u, r):
                pool.wait_ge(adj_loaded[r % 4], transfers4(u, r))
                if exists(u - 1):
                    pool.wait_ge(adjm_lo_done, u)
                a = adjt[r % 4]
                nc.gpsimd.tensor_tensor(
                    adjm[:, :].rearrange("p (g n) -> p g n", g=2),
                    a[:, 0:PAIR_N].rearrange("p (g n) -> p g n", g=2),
                    a[:, PAIR_N:ADJ_COLS].unsqueeze(2).broadcast_to([128, 2, NODES]), ALU.mult)\
                    .then_inc(adjm_done, 1)

            def split_adjm(u, r):
                pool.wait_ge(adjm_hi_done, u + 1)
                nc.gpsimd.tensor_tensor(adjm_lo[r % 2][:, :], adjm[:, :],
                                        adjm_hi[r % 2][:, :].bitcast(F32), ALU.subtract).then_inc(adjm_lo_done, 1)

            def slot(t, r):
                if exists(t + 3):
                    pool.wait_ge(xt_hi_done, t + 4)
                    nc.gpsimd.tensor_tensor(
                        xt_lo[(r + 3) % 2][:, :, :, :].rearrange("p t g n -> p (t g n)"), xt_raw[(r + 3) % 2][:, :],
                        xt_hi[(r + 3) % 2][:, :, :, :].rearrange("p t g n -> p (t g n)").bitcast(F32), ALU.subtract)\
                        .then_inc(xt_lo_done, 1)
                if exists(t + 3):
                    mask_adj(t + 3, r + 3)
                if exists(t + 1) or exists(t - 2):
                    pool.wait_ge(var_eps_done, norms(t))
                    if exists(t):
                        pool.wait_ge(x1_done, t + 1)
                    if exists(t - 3):
                        pool.wait_ge(out_done, t - 2)
                    nc.gpsimd.tensor_tensor(rstd[:, :], var_eps[:, :], minus_half[:, :], ALU.pow).then_inc(rstd_done, 1)
                if exists(t + 3) and r + 3 >= 2:
                    pool.wait_ge(x_hi_done, t + 4)
                    nc.gpsimd.tensor_tensor(x_lo[(r + 3) % 2][:, :], x_raw[(r + 3) % 4][:, :],
                                            x_hi[(r + 3) % 2][:, :].bitcast(F32), ALU.subtract)
                if exists(t + 3):
                    split_adjm(t + 3, r + 3)
                if exists(t):
                    pool.wait_ge(x1_done, t + 1)
                    if isinstance(t, int) and t == 0:
                        pool.wait_ge(bv_loaded, 16)
                    nc.gpsimd.tensor_tensor(
                        x1b[r % 2][:, :].rearrange("p (g d) -> p g d", g=2),
                        x1[r % 2][:, :].rearrange("p (g d) -> p g d", g=2),
                        bv_all[:, :].unsqueeze(1).broadcast_to([128, 2, DIM]), ALU.add).then_inc(x1b_done, 1)

            nc.gpsimd.memset(ident[:, :], 0.0).then_inc(ident_zeroed, 1)
            nc.gpsimd.memset(minus_half[:, :], -0.5)
            nc.gpsimd.memset(wv1_hi[:, :, DIM:VAL_COLS].bitcast(F32), 0.0)
            nc.gpsimd.memset(wv1_lo[:, :, DIM:VAL_COLS].bitcast(F32), 0.0)
            nc.gpsimd.memset(val[:, :, DIM:DIM + 1], 1.0)
            nc.gpsimd.memset(val[:, :, DIM + 1:VAL_COLS], 0.0).then_inc(consts_ready, 1)
            pool.wait_ge(ident_zeroed, 1)
            nc.gpsimd.affine_select(out=ident[:, :], in_=ident[:, :], compare_op=ALU.not_equal, fill=1.0, base=0,
                                    pattern=[[-1, 128]], channel_multiplier=1).then_inc(ident_ready, 1)
            pool.wait_ge(consts_ready, 1)
            mask_adj(0, 0)
            split_adjm(0, 0)
            slots(pool, slot)

        @block.scalar
        def _(act):
            def copy_agg(u, g):
                act.wait_ge(y_done[g], u + 1)
                if exists(u - 1):
                    act.wait_ge(w_done[g], u)
                nc.scalar.copy(agg[:, g, :], agg_ps[:, g, :]).then_inc(agg_copied[g], 1)

            def split_xt(u, r):
                act.wait_ge(xt_loaded[r % 2], transfers2(u, r))
                if exists(u - 2):
                    act.wait_ge(v0_done, u - 1)
                nc.scalar.copy(xt_hi[r % 2][:, :, :, :].rearrange("p t g n -> p (t g n)"),
                               xt_raw[r % 2][:, :]).then_inc(xt_hi_done, 1)

            def split_x(u, r):
                act.wait_ge(x_loaded[r % 4], transfers4(u, r))
                nc.scalar.copy(x_hi[r % 2][:, :], x_raw[r % 4][:, :]).then_inc(x_hi_done, 1)

            def split_adjm(u, r):
                act.wait_ge(adjm_done, u + 1)
                nc.scalar.copy(adjm_hi[r % 2][:, :], adjm[:, :]).then_inc(adjm_hi_done, 1)

            def norm(out, in_, first, done):
                for g in range(2):
                    n = first + g
                    last = nc.scalar.activation(out[:, graph(g)], in_[:, graph(g)], ACT.Identity,
                                                bias=shift[:, n:n + 1], scale=rstd[:, n:n + 1])
                last.then_inc(done, 1)

            def norm1(u, r):
                if exists(u):
                    act.wait_ge(shift_done, norms(u - 1))
                    if exists(u - 2):
                        act.wait_ge(x1b_done, u - 1)
                    norm(x1[r % 2], x1_sum[r % 2], 0, x1_done)

            def slot(t, r):
                if exists(t - 1):
                    act.wait_ge(score_done, t)
                    act.wait_ge(score_bias_done, t)
                    if exists(t - 2):
                        act.wait_ge(edge_done, t - 1)
                    for g in range(2):
                        last = nc.scalar.activation(exp_s[:, graph(g, NODES)], score_ps[:, g, :], ACT.Exp,
                                                    bias=score_bias[:, g:g + 1])
                    last.then_inc(score_exp_done, 1)
                if exists(t):
                    act.wait_ge(x1t_done, t + 1)
                    nc.scalar.copy(x1t[:, :, :, :], x1t_ps).then_inc(x1t_copied, 1)
                if exists(t + 3):
                    split_xt(t + 3, r + 3)
                if exists(t + 2):
                    copy_agg(t + 2, 0)
                if exists(t + 3):
                    split_x(t + 3, r + 3)
                if exists(t + 2):
                    copy_agg(t + 2, 1)
                if exists(t - 3):
                    act.wait_ge(shift_done, norms(t) - 1)
                    norm(x2[(r - 3) % 4], x2[(r - 3) % 4], 2, out_done)
                if exists(t + 3):
                    split_adjm(t + 3, r + 3)
                if r == -2:
                    act.wait_ge(params1_loaded, 16)
                    act.wait_ge(consts_ready, 1)
                    nc.scalar.copy(wv1_hi[:, :, 0:DIM], wv1T).then_inc(wv1_hi_done, 1)
                if exists(t):
                    act.wait_ge(z_done, t + 1)
                    for m in range(HALVES):
                        last = nc.scalar.activation(z[:, m, :], z_ps[:, m, :], ACT.Identity, bias=z_bias[:, m:m + 1])
                    last.then_inc(z_copied, 1)
                if r < 0:
                    norm1(t + 1, r + 1)
                if exists(t + 2):
                    act.wait_ge(row_max_done, t + 3)
                    nc.scalar.activation(exp_row[:, :], w_row_ps, ACT.Exp, bias=neg_max[:, 0:1],
                                         accum_out=exp_sum[:, 0:1]).then_inc(row_exp_done, 1)
                if r == -2:
                    act.wait_ge(at_done, 1)
                    nc.scalar.copy(at_hi[:, :, :], at_ps).then_inc(at_hi_done, 1)
                if r == -1:
                    act.wait_ge(bias_done, 1)
                    nc.scalar.copy(wv1_hi[:, :, DIM], bias_ps[:, 2:4]).then_inc(bias_hi_done, 1)
                    act.wait_ge(w1_lo_done, 1)
                if r >= 0:
                    norm1(t + 1, r + 1)
                if exists(t):
                    act.wait_ge(val_done, t + 1)
                    nc.scalar.copy(val[:, :, 0:DIM], val_ps[:, :, 0:DIM]).then_inc(val_copied, 1)

            split_adjm(0, 0)
            split_xt(0, 0)
            split_x(0, 0)
            act.wait_ge(m0_done, 1)
            nc.scalar.activation(w0_hi[:, :, 0:DIM], m0_ps, ACT.Copy, scale=ATT_SCALE).then_inc(m0_hi_done, 1)
            act.wait_ge(wv0_loaded, 16)
            nc.scalar.copy(w0_hi[:, :, DIM:2 * DIM], wv0).then_inc(wv0_hi_done, 1)
            slots(act, slot)

        @block.vector
        def _(dve):
            def weight(u, r, g):
                dve.wait_ge(agg_copied[g], u + 1)
                if exists(u - 1):
                    dve.wait_ge(w_row_done, u)
                nc.vector.tensor_tensor_reduce(agg[:, g, :], y_ps[:, g, :], agg[:, g, :],
                                               adjt[r % 4][:, PAIR_N + g:PAIR_N + g + 1], 0.0, ALU.mult, ALU.add,
                                               w_col[:, g:g + 1]).then_inc(w_done[g], 1)

            def split_x(u, r):
                dve.wait_ge(x_hi_done, u + 1)
                nc.vector.tensor_tensor(x_lo[r % 2][:, :], x_raw[r % 4][:, :], x_hi[r % 2][:, :].bitcast(F32),
                                        ALU.subtract).then_inc(first_x_lo_done, 1)

            def slot(t, r):
                if exists(t + 1):
                    dve.wait_ge(v0_done, t + 2)
                    if exists(t - 1):
                        dve.wait_ge(x1_done, t)
                    dve.wait_ge(p_copied, t + 2)
                    for g in range(2):
                        last = nc.vector.scalar_tensor_tensor(
                            out=x1_sum[(r + 1) % 2][:, graph(g)], in0=v0_ps[:, g, :], scalar=p_col[:, g:g + 1],
                            in1=x_raw[(r + 1) % 4][:, graph(g)], op0=ALU.mult, op1=ALU.add)
                    last.then_inc(x1_sum_done, 1)
                if exists(t - 1):
                    dve.wait_ge(score_exp_done, t)
                    if exists(t - 2):
                        dve.wait_ge(sum_done, t - 1)
                    nc.vector.tensor_tensor(edge[:, :], exp_s[:, :], adjt[(r - 1) % 4][:, 0:PAIR_N], ALU.mult)\
                        .then_inc(edge_done, 1)
                if exists(t):
                    dve.wait_ge(x1t_copied, t + 1)
                    nc.vector.tensor_copy(x1t_hi[:, :, :, :], x1t[:, :, :, :]).then_inc(x1t_hi_done, 1)
                if exists(t):
                    dve.wait_ge(x1t_hi_done, t + 1)
                    nc.vector.tensor_tensor(x1t_lo[:, :, :, :], x1t[:, :, :, :], x1t_hi[:, :, :, :].bitcast(F32),
                                            ALU.subtract).then_inc(x1t_lo_done, 1)
                if exists(t + 1):
                    dve.wait_ge(x1_sum_done, t + 2)
                    for g in range(2):
                        last = nc.vector.bn_stats(stats1[:, g, :], x1_sum[(r + 1) % 2][:, graph(g)])
                    last.then_inc(stats1_done, 1)
                if exists(t + 1) or exists(t - 2):
                    dve.wait_ge(norms_ready, 1)
                    if exists(t):
                        dve.wait_ge(shift_done, norms(t) - 1)
                    if exists(t + 1):
                        dve.wait_ge(stats1_done, t + 2)
                    if exists(t - 2):
                        dve.wait_ge(stats2_done, t - 1)
                    for g in range(2):
                        if exists(t + 1):
                            last = nc.vector.bn_aggr(mean_var[:, g, :], stats1[:, g, :])
                        if exists(t - 2):
                            last = nc.vector.bn_aggr(mean_var[:, 2 + g, :], stats2[:, g, :])
                    last.then_inc(mean_var_done, 1)
                    dve.wait_ge(mean_var_done, norms(t))
                    nc.vector.tensor_scalar(var_eps[:, :], mean_var[:, :, 1], EPS, None, ALU.add).then_inc(var_eps_done, 1)
                if exists(t + 2):
                    for g in range(2):
                        weight(t + 2, r + 2, g)
                if exists(t - 1):
                    dve.wait_ge(sum_done, t)
                    nc.vector.reciprocal(den_inv[:, :], sum_ps[:, :, DIM]).then_inc(den_inv_done, 1)
                    dve.wait_ge(x1b_done, t)
                    dve.wait_ge(out_stored[(r - 1) % 4], transfers4(t - 1, r - 1))
                    dve.wait_ge(den_inv_done, t)
                    for g in range(2):
                        last = nc.vector.scalar_tensor_tensor(
                            out=x2[(r - 1) % 4][:, graph(g)], in0=sum_ps[:, g, 0:DIM], scalar=den_inv[:, g:g + 1],
                            in1=x1b[(r - 1) % 2][:, graph(g)], op0=ALU.mult, op1=ALU.add)
                    last.then_inc(x2_done, 1)
                if exists(t + 1) or exists(t - 2):
                    dve.wait_ge(rstd_done, norms(t))
                    nc.vector.scalar_tensor_tensor(out=shift[:, :], in0=mean_var[:, :, 0], scalar=-1.0, in1=rstd[:, :],
                                                   op0=ALU.mult, op1=ALU.mult).then_inc(shift_done, 1)
                if r == -1:
                    dve.wait_ge(wv1_hi_done, 1)
                    nc.vector.tensor_tensor(wv1_lo[:, :, 0:DIM], wv1T, wv1_hi[:, :, 0:DIM].bitcast(F32), ALU.subtract)
                    dve.wait_ge(at_hi_done, 1)
                    nc.vector.tensor_tensor(at_lo[:, :, :], at_ps, at_hi[:, :, :].bitcast(F32), ALU.subtract)
                if exists(t + 2):
                    dve.wait_ge(w_row_done, t + 3)
                    nc.vector.tensor_reduce(neg_max[:, :], w_row_ps, AX.X, ALU.max, negate=True).then_inc(row_max_done, 1)
                if r == -2:
                    split_x(1, 1)
                if exists(t + 2):
                    dve.wait_ge(row_exp_done, t + 3)
                    nc.vector.reciprocal(inv_sum[:, :], exp_sum[:, :]).then_inc(inv_sum_done, 1)
                    dve.wait_ge(inv_sum_done, t + 3)
                    nc.vector.tensor_scalar(inv_diag[:, :], ident[0:2, 0:2], inv_sum[:, 0:1], None, ALU.mult)\
                        .then_inc(inv_diag_done, 1)
                if r == -1:
                    dve.wait_ge(bias_hi_done, 1)
                    nc.vector.tensor_tensor(wv1_lo[:, :, DIM], bias_ps[:, 2:4], wv1_hi[:, :, DIM].bitcast(F32), ALU.subtract)
                    nc.vector.tensor_copy(z_bias[:, :], bias_ps[:, 0:2])
                    nc.vector.tensor_copy(s_bias[:, :], bias_ps[:, 4:5]).then_inc(w1_lo_done, 1)
                    dve.wait_ge(w1_lo_done, 1)
                if exists(t - 1):
                    dve.wait_ge(x2_done, t)
                    for g in range(2):
                        last = nc.vector.bn_stats(stats2[:, g, :], x2[(r - 1) % 4][:, graph(g)])
                    last.then_inc(stats2_done, 1)
                if exists(t + 2):
                    dve.wait_ge(p_col_done, t + 3)
                    if exists(t + 1):
                        dve.wait_ge(x1_sum_done, t + 2)
                    nc.vector.tensor_copy(p_col[:, :], p_col_ps).then_inc(p_copied, 1)
                if exists(t):
                    dve.wait_ge(val_copied, t + 1)
                    nc.vector.tensor_scalar(score_bias[:, :], val_ps[:, :, DIM], s_bias[:, 0:1], None, ALU.add)\
                        .then_inc(score_bias_done, 1)

            nc.vector.memset(mean_var[:, :, :], 1.0).then_inc(norms_ready, 1)
            dve.wait_ge(xt_hi_done, 1)
            nc.vector.tensor_tensor(xt_lo[0][:, :, :, :].rearrange("p t g n -> p (t g n)"), xt_raw[0][:, :],
                                    xt_hi[0][:, :, :, :].rearrange("p t g n -> p (t g n)").bitcast(F32), ALU.subtract)\
                .then_inc(first_xt_lo_done, 1)
            split_x(0, 0)
            dve.wait_ge(m0_hi_done, 1)
            nc.vector.scalar_tensor_tensor(
                out=w0_lo[:, :, 0:DIM], in0=m0_ps, scalar=ATT_SCALE,
                in1=w0_hi[:, :, 0:DIM].bitcast(F32), op0=ALU.mult, op1=ALU.subtract).then_inc(m0_lo_done, 1)
            dve.wait_ge(wv0_hi_done, 1)
            nc.vector.tensor_tensor(w0_lo[:, :, DIM:2 * DIM], wv0, w0_hi[:, :, DIM:2 * DIM].bitcast(F32), ALU.subtract)\
                .then_inc(wv0_lo_done, 1)
            dve.wait_ge(params1_loaded, 16)
            nc.vector.tensor_copy(bq_wide[:, :, :], bq.unsqueeze(2).broadcast_to([128, HALVES, 128])).then_inc(bq_widened, 1)
            dve.wait_ge(norms_ready, 1)
            dve.wait_ge(ident_ready, 1)
            slots(dve, slot)

        @block.tensor
        def _(pe):
            def split_product(out, parts):
                for n, (s_hi, s_lo, m_hi, m_lo) in enumerate(parts):
                    nc.tensor.matmul(out, s_hi, m_hi, start=(n == 0), stop=False)
                    nc.tensor.matmul(out, s_hi, m_lo, start=False, stop=False)
                    mm = nc.tensor.matmul(out, s_lo, m_hi, start=False, stop=(n == len(parts) - 1))
                return mm

            def layer0(u, r, g):
                pe.wait_ge(adjm_lo_done, u + 1)
                if exists(u - 1):
                    pe.wait_ge(w_done[g], u)
                    pe.wait_ge(p_copied, u)
                if r < 2:
                    pe.wait_ge(first_xt_lo_done, 1)
                    pe.wait_ge(first_x_lo_done, u + 1)
                n = graph(g, NODES)
                split_product(agg_ps[:, g, :], [(adjm_hi[r % 2][:, n], adjm_lo[r % 2][:, n],
                                                 x_hi[r % 2][:, graph(g)], x_lo[r % 2][:, graph(g)])])
                if r == 0:
                    pe.wait_ge(m0_lo_done, 1)
                split_product(y_ps[:, g, :], [(xt_hi[r % 2][:, k, g, :], xt_lo[r % 2][:, k, g, :],
                                               w0_hi[:, k, 0:DIM], w0_lo[:, k, 0:DIM]) for k in range(HALVES)])\
                    .then_inc(y_done[g], 1)

            def fold_scores():
                pe.wait_ge(params1_loaded, 16)
                for m in range(HALVES):
                    for k in range(HALVES):
                        mm = nc.tensor.matmul(at_ps[:, m, :], wk1[:, k, m * 128:(m + 1) * 128], wq1[:, k, :],
                                              start=(k == 0), stop=(k == HALVES - 1))
                mm.then_inc(at_done, 1)

            def fold_biases():
                for n, (w, b) in enumerate(((wq1, bk), (wk1, bq))):
                    for m in range(HALVES):
                        for k in range(HALVES):
                            nc.tensor.matmul(bias_ps[:, 2 * n + m:2 * n + m + 1], w[:, k, m * 128:(m + 1) * 128],
                                             b[:, k:k + 1], start=(k == 0), stop=(k == HALVES - 1))
                pe.wait_ge(bq_widened, 1)
                for k in range(HALVES):
                    mm = nc.tensor.matmul(bias_ps[:, 4:5], bq_wide[:, k, :], bk[:, k:k + 1], start=(k == 0), stop=(k == HALVES - 1))
                mm.then_inc(bias_done, 1)

            def slot(t, r):
                if exists(t):
                    pe.wait_ge(x1_done, t + 1)
                    if exists(t - 1):
                        pe.wait_ge(z_copied, t)
                    for g in range(2):
                        for k in range(HALVES):
                            c = g * DIM + k * 128
                            mm = nc.tensor.transpose(x1t_ps[:, k, g, :], x1[r % 2][:, c:c + 128], ident[:, :])
                    mm.then_inc(x1t_done, 1)
                if exists(t + 2):
                    for g in range(2):
                        layer0(t + 2, r + 2, g)
                if r == -2:
                    fold_scores()
                if r == -1:
                    fold_biases()
                if exists(t - 1):
                    pe.wait_ge(edge_done, t)
                    pe.wait_ge(val_copied, t)
                    for g in range(2):
                        mm = nc.tensor.matmul(sum_ps[:, g, 0:VAL_COLS], edge[:, graph(g, NODES)], val[:, g, :],
                                              start=True, stop=True)
                    mm.then_inc(sum_done, 1)
                if exists(t):
                    pe.wait_ge(x1t_lo_done, t + 1)
                    if r == 0:
                        pe.wait_ge(w1_lo_done, 1)
                    for m in range(HALVES):
                        c = slice(m * 128, (m + 1) * 128)
                        mm = split_product(z_ps[:, m, :], [(
                            at_hi[:, k, c], at_lo[:, k, c], x1t_hi[:, k, :, :].rearrange("p g n -> p (g n)"),
                            x1t_lo[:, k, :, :].rearrange("p g n -> p (g n)")) for k in range(HALVES)])
                    mm.then_inc(z_done, 1)
                    for g in range(2):
                        mm = split_product(val_ps[:, g, 0:VAL_COLS], [(
                            x1t_hi[:, k, g, :], x1t_lo[:, k, g, :], wv1_hi[:, k, :], wv1_lo[:, k, :])
                            for k in range(HALVES)])
                    mm.then_inc(val_done, 1)
                if exists(t + 2):
                    for g in range(2):
                        pe.wait_ge(w_done[g], t + 3)
                    nc.tensor.transpose(w_row_ps, w_col[:, :], ident[:, :]).then_inc(w_row_done, 1)
                    if r + 2 == 0:
                        pe.wait_ge(wv0_lo_done, 1)
                    if exists(t + 1):
                        pe.wait_ge(x1_sum_done, t + 2)
                    for g in range(2):
                        mm = split_product(v0_ps[:, g, :], [(
                            xt_hi[r % 2][:, k, g, :], xt_lo[r % 2][:, k, g, :],
                            w0_hi[:, k, DIM:2 * DIM], w0_lo[:, k, DIM:2 * DIM]) for k in range(HALVES)])
                    mm.then_inc(v0_done, 1)
                for g in range(2):
                    if exists(t):
                        if g == 0:
                            pe.wait_ge(z_copied, t + 1)
                            if exists(t - 1):
                                pe.wait_ge(x2_done, t)
                        for k in range(HALVES):
                            mm = nc.tensor.matmul(score_ps[:, g, :], z[:, k, graph(g, NODES)], x1t[:, k, g, :],
                                                  start=(k == 0), stop=(k == HALVES - 1))
                        if g == 1:
                            mm.then_inc(score_done, 1)
                    if g == 0 and exists(t + 2):
                        pe.wait_ge(inv_diag_done, t + 3)
                        nc.tensor.matmul(p_col_ps, exp_row[:, :], inv_diag[:, :], start=True, stop=True)\
                            .then_inc(p_col_done, 1)

            pe.wait_ge(ident_ready, 1)
            for _ in range(WARM_UP):
                nc.tensor.matmul(ps[:, 0, 0:128], ident[:, :], ident[:, :], start=True, stop=True)
            pe.wait_ge(wqk_loaded, 16)
            for m in range(HALVES):
                for k in range(HALVES):
                    mm = nc.tensor.matmul(m0_ps[:, m, :], wqkT[:, k, m * 128:(m + 1) * 128], wqkT[:, 2 + k, :],
                                          start=(k == 0), stop=(k == HALVES - 1))
            mm.then_inc(m0_done, 1)
            slots(pe, slot)


def kernel(**inputs):
    import numpy as np
    import concourse.bacc as bacc
    from concourse.bass_utils import run_bass_kernel_spmd

    a = {name: np.asarray(value) for name, value in inputs.items()}

    def rows(w):
        return w.reshape(-1, 128, w.shape[-1]).transpose(1, 0, 2).reshape(128, -1)

    x = a["x"].reshape(PAIRS, 2, NODES, HALVES, 128)
    adjt = a["adj"].reshape(PAIRS, 2, NODES, NODES).transpose(0, 3, 1, 2).reshape(PAIRS, NODES, PAIR_N)
    mask = a["nodemask"].reshape(PAIRS, 2, NODES).transpose(0, 2, 1)
    arrays = {
        "x_pairs": x.transpose(0, 2, 1, 3, 4).reshape(PAIRS, NODES, PAIR_X),
        "xt_pairs": x.transpose(0, 4, 3, 1, 2).reshape(PAIRS, 128, PAIR_X),
        "adjt_pairs": np.concatenate([adjt, mask], axis=2),
        "params0": np.concatenate([rows(a["L0_gnn_Wqk"].T), rows(a["L0_gnn_Wv"])], axis=1),
        "params1": np.concatenate([rows(a["L1_gnn_Wq_w"]), rows(a["L1_gnn_Wk_w"]), rows(a["L1_gnn_Wv_w"].T),
                                   rows(a["L1_gnn_Wq_b"][:, None]), rows(a["L1_gnn_Wk_b"][:, None])], axis=1),
        "value_bias": a["L1_gnn_Wv_b"],
    }
    arrays = {name: np.ascontiguousarray(value) for name, value in arrays.items()}
    nc = bacc.Bacc("TRN2", target_bir_lowering=False, num_devices=1)
    args = [nc.dram_tensor(name, value.shape, F32, kind="ExternalInput").ap() for name, value in arrays.items()]
    out = nc.dram_tensor("out_pairs", (PAIRS, NODES, PAIR_X), F32, kind="ExternalOutput").ap()
    build(nc, *args, out)
    result = run_bass_kernel_spmd(nc, [arrays], core_ids=[0]).results[0]["out_pairs"]
    return result.reshape(PAIRS, NODES, 2, DIM).transpose(0, 2, 1, 3).reshape(GRAPHS, NODES, DIM)
```
